# Optimizing a Trainium2 kernel written in Bass

```python
import numpy as np
import jax
import jax.numpy as jnp

def _softmax(x, axis=-1):
    return jax.nn.softmax(x, axis=axis)

def _gelu(x):
    return jax.nn.gelu(x, approximate=True)

def _silu(x):
    return jax.nn.silu(x)

def _sigmoid(x):
    return jax.nn.sigmoid(x)

def _layernorm(x, axis=-1, eps=1e-05):
    m = jnp.mean(x, axis=axis, keepdims=True)
    v = jnp.var(x, axis=axis, keepdims=True)
    return (x - m) / jnp.sqrt(v + eps)

def _scatter_add(tgt, idx, src, axis=0):
    return tgt.at[idx].add(src)

def _segment_sum(src, seg, n):
    return jax.ops.segment_sum(src, seg, n)
kernel_name = 'mk_vit_tower_d1_tok_img768_r4_7cfedf'

def setup_inputs(seed: int=0):
    np.random.seed(seed)
    _w = jnp.asarray

    def _rec_inputs():
        import jax
        import jax.numpy as jnp
        _rk = jax.random.key(seed)
        x = -0.000147625 + 0.999875 * jax.random.normal(jax.random.fold_in(_rk, 1), (64, 12, 224, 224), jnp.float32)
        return x
    x = _rec_inputs()

    def _L0_tok_setup():
        import jax, jax.numpy as jnp
        import numpy as np
        IMG = 224
        PATCH = 16
        EMBED = 192
        C = 12
        B = 64
        key = jax.random.key(seed)
        k1, k2 = jax.random.split(key)
        x = jax.random.normal(k1, (B, C, IMG, IMG), dtype=jnp.float32)
        channel_weights = jax.random.normal(k2, (C, EMBED), dtype=jnp.float32)
        return {'x': x, 'channel_weights': channel_weights}
    _L0_tok_all = _L0_tok_setup()
    _L0_tok_in = {k: v for k, v in _L0_tok_all.items() if k in ('channel_weights',)}
    del _L0_tok_all

    def _L0_attn_setup():
        import jax, jax.numpy as jnp
        import numpy as np
        import math
        DIM = 192
        NUM_HEADS = 12
        HEAD_DIM = DIM // NUM_HEADS
        ORDER = 2
        SCALE = HEAD_DIM ** (-0.5)
        key = jax.random.key(seed)
        ks = jax.random.split(key, 5)
        B, N, C = (8, 256, DIM)
        x = jax.random.normal(ks[0], (B, N, C), dtype=jnp.float32)
        w_qkv = jax.random.normal(ks[1], (C, 3 * C), dtype=jnp.float32) * C ** (-0.5)
        w_proj = jax.random.normal(ks[2], (C, C), dtype=jnp.float32) * C ** (-0.5)
        b_proj = jax.random.normal(ks[3], (C,), dtype=jnp.float32) * 0.02
        return {'x': x, 'w_qkv': w_qkv, 'w_proj': w_proj, 'b_proj': b_proj}
    _L0_attn_all = _L0_attn_setup()
    _L0_attn_in = {k: v for k, v in _L0_attn_all.items() if k in ('w_qkv', 'w_proj', 'b_proj')}
    del _L0_attn_all

    def _L0_ffn_setup():
        import jax, jax.numpy as jnp
        import numpy as np
        E, C, F, K = (8, 192, 768, 2)
        key = jax.random.key(seed)
        k0, k1, k2, k3 = jax.random.split(key, 4)
        B, T = (8, 512)
        return {'x': jax.random.normal(k0, (B, T, C), jnp.float32), 'router_w': jax.random.normal(k1, (E, C), jnp.float32) * 0.02, 'w1': jax.random.normal(k2, (E, C, F), jnp.float32) * 0.02, 'b1': jnp.zeros((E, F), jnp.float32), 'w2': jax.random.normal(k3, (E, F, C), jnp.float32) * 0.02, 'b2': jnp.zeros((E, C), jnp.float32)}
    _L0_ffn_all = _L0_ffn_setup()
    _L0_ffn_in = {k: v for k, v in _L0_ffn_all.items() if k in ('router_w', 'w1', 'b1', 'w2', 'b2')}
    del _L0_ffn_all
    return {'x': x, 'L0_tok_channel_weights': _L0_tok_in['channel_weights'], 'L0_attn_w_qkv': _L0_attn_in['w_qkv'], 'L0_attn_w_proj': _L0_attn_in['w_proj'], 'L0_attn_b_proj': _L0_attn_in['b_proj'], 'L0_ffn_router_w': _L0_ffn_in['router_w'], 'L0_ffn_w1': _L0_ffn_in['w1'], 'L0_ffn_b1': _L0_ffn_in['b1'], 'L0_ffn_w2': _L0_ffn_in['w2'], 'L0_ffn_b2': _L0_ffn_in['b2']}

def reference(x, L0_tok_channel_weights, L0_attn_w_qkv, L0_attn_w_proj, L0_attn_b_proj, L0_ffn_router_w, L0_ffn_w1, L0_ffn_b1, L0_ffn_w2, L0_ffn_b2):
    import jax
    import jax.numpy as jnp

    def _L0_tok_ref(x, channel_weights):
        import jax, jax.numpy as jnp
        import numpy as np
        IMG = 224
        PATCH = 16
        EMBED = 192
        C = 12
        B = 64
        Bb, Cc, H, W = x.shape
        K = PATCH
        n = H // K
        pooled = x.reshape(Bb, Cc, n, K, n, K).sum(axis=(3, 5))
        out = jnp.einsum('bcij,ce->bije', pooled, channel_weights)
        return out.reshape(Bb, n * n, EMBED)

    def _L0_attn_ref(x, w_qkv, w_proj, b_proj):
        import jax, jax.numpy as jnp
        import numpy as np
        import math
        DIM = 192
        NUM_HEADS = 12
        HEAD_DIM = DIM // NUM_HEADS
        ORDER = 2
        SCALE = HEAD_DIM ** (-0.5)
        B, N, C = x.shape
        H, Dh = (NUM_HEADS, HEAD_DIM)
        qkv = (x @ w_qkv).reshape(B, N, 3, H, Dh)
        qkv = jnp.transpose(qkv, (2, 0, 3, 1, 4))
        q, k, v = (qkv[0], qkv[1], qkv[2])
        q = q * SCALE
        qk = jnp.einsum('bhnd,bhmd->bhnm', q, k)
        attn = jnp.ones_like(qk)
        x_power = qk
        for i in range(1, ORDER + 1):
            attn = attn + x_power / math.factorial(i)
            if i < ORDER:
                x_power = x_power * qk
        attn = jax.nn.relu(attn)
        attn = attn / jnp.sum(attn, axis=-1, keepdims=True)
        out = jnp.einsum('bhnm,bhmd->bhnd', attn, v)
        out = jnp.transpose(out, (0, 2, 1, 3)).reshape(B, N, C)
        return out @ w_proj + b_proj

    def _L0_ffn_ref(x, router_w, w1, b1, w2, b2):
        import jax, jax.numpy as jnp
        import numpy as np
        E, C, F, K = (8, 192, 768, 2)
        B, T, Cc = x.shape
        flat = x.reshape(-1, Cc)
        logits = flat @ router_w.T
        probs = jax.nn.softmax(logits.astype(jnp.float32), axis=-1)
        top_w, top_i = jax.lax.top_k(probs, K)
        top_w = (top_w / top_w.sum(-1, keepdims=True)).astype(x.dtype)
        out = jnp.zeros_like(flat)
        for e in range(E):
            w_e = jnp.sum(top_w * (top_i == e), axis=-1)[:, None]
            h = jax.nn.gelu(flat @ w1[e] + b1[e], approximate=False)
            out = out + w_e * (h @ w2[e] + b2[e])
        return out.reshape(B, T, Cc)
    h = _L0_tok_ref(x, L0_tok_channel_weights)
    h = h + _L0_attn_ref(_layernorm(h, axis=-1), L0_attn_w_qkv, L0_attn_w_proj, L0_attn_b_proj)
    h = h + _L0_ffn_ref(_layernorm(h, axis=-1), L0_ffn_router_w, L0_ffn_w1, L0_ffn_b1, L0_ffn_w2, L0_ffn_b2)
    return h

_drawn_inputs = setup_inputs


def setup_inputs(seed=0):
    import zlib

    import numpy as np

    out = dict(_drawn_inputs(seed))
    spreads = {'L0_ffn_b1': (0.0, 0.8), 'L0_ffn_b2': (0.0, 2.0)}
    factors = {'L0_attn_w_qkv': 8.0,
     'L0_attn_w_proj': 8.0,
     'L0_attn_b_proj': 172.344,
     'L0_ffn_router_w': 8.0,
     'L0_ffn_w1': 8.0,
     'L0_ffn_w2': 8.0}
    for name, (base, spread) in spreads.items():
        noise = np.random.default_rng([zlib.crc32(name.encode()), seed]).standard_normal(out[name].shape)
        drawn = base * np.exp(spread * noise) if base else spread * noise
        out[name] = jnp.asarray(drawn.astype(out[name].dtype))
    for name, factor in factors.items():
        out[name] = (out[name] * factor).astype(out[name].dtype)
    return out
```

```python
from contextlib import ExitStack

import numpy as np

import concourse.bass as bass
from concourse import mybir

ALU = mybir.AluOpType
ACT = mybir.ActivationFunctionType
F32 = mybir.dt.float32
BF16 = mybir.dt.bfloat16
I32 = mybir.dt.int32
U32 = mybir.dt.uint32
AX = mybir.AxisListType

B, C, IMG, PATCH = 64, 12, 224, 16
G = IMG // PATCH
NTOK = G * G
E = 192
HEADS, HD = 12, 16
NE, FF = 8, 768
EPS = 1e-5

IPS = 4
STEPS = B // IPS
TOK = NTOK // 2
NT = 2 * IPS
ROWP = IMG // 2
CPAD = 32
U = C + 1
NF = U * (U + 1) // 2
FOFF = [sum(U - a for a in range(i)) for i in range(U)]
HV = HD + 1
NV = HEADS * HV
ATT = E + U
KA = (ATT + 1) // 2
KB = ATT - KA
RES = E + NE
ROW = E + NE + 1
T = 512
TP = T // 128
MC = FF // 128
KH = E // 2
TOKENS = B * NTOK
CAP = TOKENS + T
IDLE = NE * CAP
CHUNKS = 2 * IPS
XSLOTS = 4
CH = C // 2
TILES_PER_STEP = 3
PRO = 4
TILES = 57
TAIL = (TILES - (STEPS - PRO) * TILES_PER_STEP) // TILES_PER_STEP
for _s in range(PRO, STEPS):
    assert 2 * NTOK * IPS * _s - T * (TILES_PER_STEP * (_s - PRO + 1)) > NE * (T - 1)
assert 2 * NTOK * IPS * (PRO - 1) > NE * (T - 1)
assert TILES * T > 2 * TOKENS + NE * (T - 1)

_C = {}
_W = 0
for _n, _w in (("ident", 128), ("rowsel", G), ("mixinit", 2 * IPS * C), ("self", 2 * NF), ("selg", 4 * NF),
               ("e00", U), ("half", NF), ("wvinit", NV), ("iota", NE), ("base", NE), ("ids", NT),
               ("tri", 128)):
    _C[_n] = (_W, _w)
    _W += _w
CONSTS = _W


def constants():
    c = np.zeros((128, CONSTS), np.float32)

    def put(name, a, rows):
        o, w = _C[name]
        c[:rows, o:o + w] = np.asarray(a, np.float32).reshape(rows, w)

    put("ident", np.eye(128), 128)
    put("rowsel", np.arange(ROWP)[:, None] // (PATCH // 2) == np.arange(G), ROWP)
    mix = np.zeros((128, 2 * IPS * C))
    for i in range(IPS):
        for k in range(C):
            mix[CPAD * i + k, C * i + k] = 1
    put("mixinit", mix, 128)
    first = np.zeros((U, NF))
    second = np.zeros((U, NF))
    once = np.ones(NF)
    for i in range(U):
        for k in range(i, U):
            f = FOFF[i] + k - i
            first[i, f] = second[k, f] = 1
            if i == k:
                once[f] = 0.5
    put("self", np.concatenate([first * once, second], 1), U)
    put("selg", np.concatenate([first * once, second, second * once, first], 1), U)
    e00 = np.zeros((U, U))
    e00[0, 0] = 1
    put("e00", e00, U)
    half = np.zeros((NF, NF))
    half[0, 0] = 0.5
    put("half", half, NF)
    wv = np.zeros((U, HEADS, HV))
    wv[0, :, HD] = 1
    put("wvinit", wv, U)
    put("iota", np.tile(np.arange(NE), (128, 1)), 128)
    put("base", np.tile(np.arange(NE) * CAP, (128, 1)), 128)
    t = np.arange(NT)
    put("ids", (t % IPS) * NTOK + (t // IPS) * TOK + np.arange(TOK)[:, None], TOK)
    put("tri", np.arange(TOK)[:, None] < np.where(np.arange(128) < TOK, np.arange(128), 0), TOK)
    pad = np.arange(TOKENS, TOKENS + T, dtype=np.int32).reshape(128, TP)
    return c, pad


ORDER = [
    "L S1 M0 S2 M1 P0 M2 P1 S3 M3 M4 S4 M5 X S5 N0 N1 S6 N2 P2 N3 A".split(),
    "L M0 S7 M1 P3 M2 S8 M3 P4 M4 M5 X R N0 P5 N1 N2 N3 A".split(),
    "L S9 Q0 M0 M1 Q1 V P6 M2 M3 Q2 M4 M5 Q3 X N0 P7 N1 N2 N3 A".split(),
]


def vit_layer(nc, x, cw, w_qkv, w_proj, b_proj, router, w1, b1, w2, b2, consts, padids, out):
    rows_d = nc.dram_tensor("rows_d", [IDLE + T, ROW], F32, kind="Internal").ap()
    b2_d = nc.dram_tensor("b2_d", [NE, 3, E], BF16, kind="Internal").ap()

    with ExitStack() as ctx:
        def sb(name, shape, dt=F32):
            return ctx.enter_context(nc.sbuf_tensor(name, shape, dt))

        def sem(name):
            return ctx.enter_context(nc.semaphore(name))

        ps = ctx.enter_context(nc.psum_tensor("ps", [128, 8, 512], F32))

        cst = sb("cst", [128, CONSTS])
        tri = sb("tri", [TOK, 128], BF16)
        ones = sb("ones", [TOK, 128], BF16)
        mix = cst[:, _C["mixinit"][0]:_C["mixinit"][0] + 2 * IPS * C]
        cws = sb("cws", [C, E])
        cwc = sb("cwc", [C, E])
        cwT = sb("cwT", [KH, 2, U])
        wqkv = sb("wqkv", [KH, 2, 3 * E])
        rts = sb("rts", [NE, E])
        rtT = sb("rtT", [KH, 2, NE])
        small = sb("small", [C, 4])
        smallr = sb("smallr", [NE, 4])
        resA = sb("resA", [KA, RES])
        resB = sb("resB", [KB, RES])
        resT = sb("resT", [KH, 4, KA])
        qk = sb("qk", [HD, 2, HEADS, U])
        amat = sb("amat", [U, HEADS, U])
        bmat = sb("bmat", [U, HEADS, 2 * NF])
        afac = sb("afac", [NF, 2, 2, NF])
        atmp = sb("atmp", [NF, 2, NF])
        score = sb("score", [NF, HEADS, NF])
        b2f = sb("b2f", [NE, 2, E])
        b2s = sb("b2s", [NE, 3, E], BF16)
        pad = sb("pad", [128, TP, ROW])
        padi = sb("padi", [128, TP], I32)
        nhalf = sb("nhalf", [TOK, NT])

        xbuf = sb("xbuf", [ROWP, XSLOTS, CH, 2 * IMG])
        red = sb("red", [ROWP, IPS, CPAD, G])
        pT = sb("pT", [128, G, G])
        prod = sb("prod", [TOK, NT, C])
        var1 = sb("var1", [TOK, NT])
        rstd1 = sb("rstd1", [TOK, NT])
        phi = sb("phi", [TOK, NT, NF])
        gts = sb("gts", [U, IPS, NF])
        phiT = sb("phiT", [NF, NT * TOK])
        gws = sb("gws", [NF, IPS, NV])
        us = sb("us", [NF, HEADS, IPS, HV])
        rden = sb("rden", [TOK, 2, HEADS])
        att = sb("att", [TOK, NT, ATT])
        attA = sb("attA", [KA, NT * TOK])
        attB = sb("attB", [KB, NT * TOK])
        h1s = sb("h1s", [TOK, NT, RES])
        stats = sb("stats", [TOK, NT, 6])
        mv = sb("mv", [TOK, NT, 2])
        var2 = sb("var2", [TOK, NT])
        rstd2 = sb("rstd2", [TOK, NT])
        top = sb("top", [TOK, NT, NE])
        topi = sb("topi", [TOK, NT, NE], U32)
        gap = sb("gap", [TOK, NT])
        th = sb("th", [TOK, NT])
        idxf = sb("idxf", [TOK, 2, NT])
        hot = sb("hot", [TOK, 2 * NT, NE])
        hotw = sb("hotw", [TOK, 2 * NT, NE])
        gk = sb("gk", [TOK, 2, NT])
        mask = sb("mask", [TOK, (NT + 1) * NE], BF16)
        ids = sb("ids", [TOK, NT])
        base = sb("base", [128, NE])
        pos = sb("pos", [TOK, NT * NE])
        slotf = sb("slotf", [TOK, 2 * NT])
        sloti = sb("sloti", [TOK, 2 * NT], I32)
        rows = sb("rows", [TOK, NT, ROW])

        endi = sb("endi", [1, NE], I32)
        cons = sb("cons", [128, NE])
        pend = sb("pend", [128, NE])
        pmax = sb("pmax", [128, NE])
        pidx = sb("pidx", [128, NE], U32)
        pick = sb("pick", [128, 8])
        hotE = sb("hotE", [128, 3, NE])
        tmpE = sb("tmpE", [128, NE])
        seli = sb("seli", [1, 2], I32)
        xr = sb("xr", [128, 3, TP, ROW])
        w1s = sb("w1s", [KH, 3, 2, FF])
        w2s = sb("w2s", [128, 3, MC, E])
        b1s = sb("b1s", [128, 3, MC])
        b2t = sb("b2t", [3, 3, E], BF16)
        xT = sb("xT", [KH, 2, T])
        hT = sb("hT", [128, MC, T])
        gmul = sb("gmul", [128, TP, NE])
        gate = sb("gate", [128, 3, TP])
        ys = sb("ys", [128, 3, TP, E])

        def const(name, rows=128):
            o, w = _C[name]
            return cst[0:rows, o:o + w]

        d_cst, d_w, d_b2, d_pad = sem("d_cst"), sem("d_w"), sem("d_b2"), sem("d_pad")
        d_x = [sem(f"d_x{i}") for i in range(XSLOTS)]
        d_h1, d_scat, d_add = sem("d_h1"), sem("d_scat"), sem("d_add")
        d_tile = [sem(f"d_tile{i}") for i in range(3)]
        SETUP = {
            "pool": ["zeros", "fills", "pad"],
            "dve": ["copies", "cwc", "router", "cwT", "rtT", "mix", "amat"]
                   + [f"score{h}" for h in range(HEADS)] + ["score", "b2"],
            "act": ["resT", "logits", "values", "qk", "bmat"] + [f"factors{h}" for h in range(HEADS)],
            "pe": ["turned", "gram", "logits", "values", "qk", "amat", "bmat"]
                  + [f"factors{h}" for h in range(HEADS)],
        }
        s_set = {e: sem(f"set_{e}") for e in SETUP}

        def given(engine, name, ins):
            ins.then_inc(s_set[engine], 1)

        def set_wait(eng, engine, name):
            eng.wait_ge(s_set[engine], SETUP[engine].index(name) + 1)

        s_dve = sem("dve_step")
        s_dvs = sem("dve_setup")
        s_dvt = sem("dve_tile")
        s_pooled = sem("pooled")
        s_psum1 = sem("rows_summed")
        s_pT = sem("pT_ready")
        s_mix = sem("mix_ready")
        s_var1, s_rstd1 = sem("var1_ready"), sem("rstd1_ready")
        s_phi = sem("phi_ready")
        s_g, s_phT = sem("moments_ready"), sem("phiT_turned")
        s_gts, s_phTs = sem("moments_copied"), sem("phiT_copied")
        s_gw, s_gws = sem("gw_ready"), sem("gw_copied")
        s_u, s_us = sem("u_ready"), sem("u_copied")
        s_num, s_att = sem("num_ready"), sem("att_ready")
        s_turn, s_tA, s_tB = sem("att_turned"), sem("attT_by_act"), sem("attT_by_dve")
        s_res, s_h1 = sem("residual_ready"), sem("residual_copied")
        s_stored = sem("residual_stored")
        s_var2, s_rstd2 = sem("var2_ready"), sem("rstd2_ready")
        s_gap, s_th = sem("gap_ready"), sem("tanh_ready")
        s_mask, s_rank = sem("mask_ready"), sem("rank_ready")
        s_slots = sem("slots_ready")
        s_listed = sem("rows_listed")
        s_pick, s_picked = sem("tile_picked"), sem("pick_read")
        s_free = sem("tile_buffers_free")
        s_xt, s_xa, s_xd = sem("rows_turned"), sem("xT_by_act"), sem("xT_by_dve")
        s_h, s_hT = sem("hidden_ready"), sem("hidden_gelu")
        s_y, s_ys = sem("y_ready"), sem("y_scaled")
        s_gate = sem("gate_ready")
        s_waits = sem("waits_passed")
        s_ends = sem("list_ends_ready")

        NUMB, TURN, RESB = (1, 2, 0, 1), (2, 0, 1, 2), (0, 1, 2, 0)
        HB, XB = (3, 4, 5, 3, 4, 5), (3, 4)

        def yout(n):
            return ps[:, 6 + n // 2, (n % 2) * E:(n % 2 + 1) * E]

        def factors(h):
            return ps[0:NF, h % 6, 0:4 * NF].rearrange("p (a b f) -> p b a f", a=2, b=2)

        def tile_landed(j, buf):
            return (j - buf) * 32 + 96

        wv3 = const("wvinit", U).rearrange("p (h v) -> p h v", h=HEADS)

        xv = x.rearrange("b c (p r) w -> b p c (r w)", r=2)
        outv = out[0:TOKENS].rearrange("(b h p) e -> b p h e", h=2, p=TOK)

        def tiles_do(eng, handlers, s=None, j=None, with_tiles=True, with_step=True, pooling=True):
            for b, names in enumerate(ORDER):
                for name in names:
                    if name in ("L", "X", "A") or name[0] in "MN":
                        if with_tiles and name[0] in handlers:
                            handlers[name[0]](j + b, b, *[int(n) for n in name[1:]])
                    elif name[0] == "P":
                        if with_step and pooling and "P" in handlers:
                            handlers["P"](s, int(name[1:]))
                    elif with_step:
                        if name[0] == "Q":
                            if "Q" in handlers:
                                handlers["Q"](s, int(name[1:]))
                        elif name in handlers:
                            handlers[name](s)

        def schedule(eng, handlers, start=None, prime=None, before_tail=None):
            with eng.Fori(0, PRO) as s:
                if start:
                    start(s)
                tiles_do(eng, handlers, s=s, with_tiles=False)
            if prime:
                prime()
            with eng.Fori(PRO, STEPS - 1) as s:
                if start:
                    start(s)
                tiles_do(eng, handlers, s=s, j=(s - PRO) * TILES_PER_STEP)
            s = STEPS - 1
            tiles_do(eng, handlers, s=s, j=(s - PRO) * TILES_PER_STEP, pooling=False)
            if before_tail:
                before_tail()
            with eng.Fori(0, TAIL) as i:
                tiles_do(eng, handlers, j=i * TILES_PER_STEP + (STEPS - PRO) * TILES_PER_STEP, with_step=False)

        def wait_first(eng, signal, value):
            eng.wait_ge(signal, value)
            eng.sem_inc(s_waits, 1)

        block = ctx.enter_context(nc.Block())

        @block.sync
        def _(sp):
            sp.dma_start(cst[:], consts).then_inc(d_cst, 16)

            def load_chunk(s, k):
                sp.dma_start(xbuf[:, k % XSLOTS],
                             xv[bass.ds(s * IPS + k // 2, 1), :, CH * (k % 2):CH * (k % 2) + CH]
                             .rearrange("b p c w -> p (b c) w")).then_inc(d_x[k % XSLOTS], 16)

            def load_first(s):
                for k in range(XSLOTS):
                    load_chunk(s, k)

            weights = [
                (cws[:], cw), (wqkv[:], w_qkv.rearrange("(h p) f -> p h f", p=KH)), (rts[:], router),
                (resA[:, 0:E], w_proj[0:KA]), (resB[0:E - KA, 0:E], w_proj[KA:E]),
                (resB[E - KA:E - KA + C, 0:E], cw),
                (resB[E - KA + C:KB, 0:E], b_proj.rearrange("(a e) -> a e", a=1)),
                (b2f[:, 0, :], b2), (padi[:], padids),
            ]
            for dst, src in weights:
                sp.dma_start(dst, src).then_inc(d_w, 16)
            load_first(0)
            for k in range(XSLOTS, CHUNKS):
                sp.wait_ge(s_pooled, k - XSLOTS + 1)
                load_chunk(0, k)

            set_wait(sp, "pool", "pad")
            sp.dma_start(rows_d[IDLE:IDLE + T].rearrange("(p n) c -> p n c", n=TP), pad[:]).then_inc(d_pad, 16)
            sp.dma_start(out[TOKENS:TOKENS + T].rearrange("(p n) c -> p n c", n=TP),
                         pad[:, :, 0:E]).then_inc(d_pad, 16)
            set_wait(sp, "dve", "b2")
            sp.dma_start(b2_d, b2s[:]).then_inc(d_b2, 16)
            sp.wait_ge(d_b2, 16)
            sp.wait_ge(d_pad, 32)

            def start(s):
                sp.wait_ge(s_pooled, s * CHUNKS + CHUNKS)
                load_first(s + 1)

            def P(s, k):
                if k < XSLOTS:
                    sp.wait_ge(s_pooled, s * CHUNKS + CHUNKS + k + 1)
                    load_chunk(s + 1, k + XSLOTS)

            def load_tile(j, buf, listed):
                wait_first(sp, s_pick, j + 1)
                e = sp.value_load(seli[0:1, 0:1], min_val=0, max_val=NE - 1)
                row = sp.value_load(seli[0:1, 1:2], min_val=0, max_val=IDLE)
                sp.sem_inc(s_picked, 1)
                sp.wait_ge(s_free, j + 1)
                sp.wait_ge(s_listed, listed)
                w = d_tile[buf]
                sp.dma_start(xr[:, buf], rows_d[bass.ds(row, T)]
                             .rearrange("(p n) c -> p n c", n=TP)).then_inc(w, 16)
                for hf in range(2):
                    sp.dma_start(w1s[:, buf, hf], w1[bass.ds(e, 1), hf * KH:(hf + 1) * KH]
                                 .rearrange("b p f -> p (b f)")).then_inc(w, 16)
                sp.dma_start(w2s[:, buf], w2[bass.ds(e, 1)]
                             .rearrange("b (m p) f -> p (b m) f", p=128)).then_inc(w, 16)
                sp.dma_start(b1s[:, buf], b1[bass.ds(e, 1)]
                             .rearrange("b p m -> p (b m)")).then_inc(w, 16)
                sp.dma_start(b2t[:, buf], b2_d[bass.ds(e, 1)]
                             .rearrange("b k c -> k (b c)")).then_inc(w, 16)

            listed = [None]

            def L(j, b):
                load_tile(j + 1, (b + 1) % 3, listed[0])

            def S9(s):
                sp.wait_ge(s_h1, s * IPS + IPS)
                for hf in range(2):
                    sp.dma_start(outv[bass.ds(s * IPS, IPS), :, hf].rearrange("b p e -> p b e"),
                                 h1s[:, hf * IPS:(hf + 1) * IPS, 0:E]).then_inc(d_h1, 16)

            def V(s):
                sp.wait_ge(d_h1, s * 32 + 32)
                sp.sem_inc(s_stored, 1)

            handlers = {"P": P, "L": L, "S9": S9, "V": V}
            with sp.Fori(0, PRO) as s:
                start(s)
                tiles_do(sp, handlers, s=s, with_tiles=False)
            load_tile(0, 0, PRO + 1)
            with sp.Fori(PRO, STEPS - 1) as s:
                start(s)
                listed[0] = s + 1
                tiles_do(sp, handlers, s=s, j=(s - PRO) * TILES_PER_STEP)
            s = STEPS - 1
            listed[0] = s + 1
            tiles_do(sp, handlers, s=s, j=(s - PRO) * TILES_PER_STEP, pooling=False)
            sp.wait_ge(s_ends, 1)
            for e in range(NE):
                end = sp.value_load(endi[0:1, e:e + 1], min_val=e * CAP,
                                    max_val=e * CAP + TOKENS)
                sp.dma_start(rows_d[bass.ds(end, T)].rearrange("(p n) c -> p n c", n=TP), pad[:]).then_inc(d_pad, 16)
            sp.wait_ge(d_pad, 32 + 16 * NE)
            listed[0] = STEPS + 1
            with sp.Fori(0, TAIL) as i:
                tiles_do(sp, handlers, j=i * TILES_PER_STEP + (STEPS - PRO) * TILES_PER_STEP, with_step=False)
            sp.wait_ge(s_free, 3 + TILES)

        @block.gpsimd
        def _(pool):
            pool.sem_inc(s_stored, 1)
            pool.sem_inc(s_listed, 1)
            pool.sem_inc(s_free, 3)
            nc.gpsimd.memset(red[:], 0.0)
            given("pool", "zeros", nc.gpsimd.memset(pad[:], 0.0))
            nc.gpsimd.memset(phi[:, :, 0:1], 1.0)
            nc.gpsimd.memset(att[:, :, ATT - 1:ATT], 1.0)
            nc.gpsimd.memset(mask[:], 0.0)
            nc.gpsimd.memset(ones[:], 1.0)
            nc.gpsimd.memset(cwT[:, :, 0:1], 0.0)
            given("pool", "fills", nc.gpsimd.memset(nhalf[:], -0.5))
            pool.wait_ge(d_w, 16 * 9)
            set_wait(pool, "pool", "zeros")
            given("pool", "pad", nc.gpsimd.tensor_copy(pad[:, :, ROW - 1:ROW].bitcast(I32), padi[:].unsqueeze(2)))

            def S2(s):
                set_wait_once(pool)
                pool.wait_ge(s_var1, s + 1)
                nc.gpsimd.tensor_tensor(rstd1[:], var1[:], nhalf[:], ALU.pow).then_inc(s_rstd1, 1)

            def set_wait_once(eng):
                set_wait(eng, "pool", "fills")

            def S8(s):
                pool.wait_ge(s_var2, s + 1)
                nc.gpsimd.tensor_tensor(rstd2[:], var2[:], nhalf[:], ALU.pow).then_inc(s_rstd2, 1)

            def Q(s, q):
                if q == 0:
                    wait_first(pool, s_slots, s + 1)
                for t in (2 * q, 2 * q + 1):
                    for k in range(2):
                        pool.indirect_dma_start(
                            rows_d, bass.IndirectOffsetOnAxis(ap=sloti[:, k * NT + t:k * NT + t + 1], axis=0),
                            rows[:, t, :], None).then_inc(d_scat, 16)
                if q == 3:
                    pool.wait_ge(d_scat, s * (32 * NT) + 32 * NT)
                    pool.wait_ge(s_stored, s + 2)
                    pool.sem_inc(s_listed, 1)

            def A(j, b):
                wait_first(pool, s_ys, j * TP + TP)
                for n in range(TP):
                    pool.indirect_dma_start(
                        out, bass.IndirectOffsetOnAxis(ap=xr[:, b, n, ROW - 1:ROW].bitcast(I32), axis=0),
                        ys[:, b, n, :], None, compute_op=ALU.add).then_inc(d_add, 16)
                pool.wait_ge(d_add, j * (16 * TP) + 16 * TP)
                pool.sem_inc(s_free, 1)

            schedule(pool, {"S2": S2, "S8": S8, "Q": Q, "A": A})

        @block.scalar
        def _(act):
            copy = nc.scalar.copy
            set_wait(act, "pe", "turned")
            turned = ps[0:KH, 1, 0:4 * KA].rearrange("p (a k) -> p a k", a=4)
            copy(resT[:, 0:2, :], turned[:, 0:2, :])
            given("act", "resT", copy(resT[:, 2:4, 0:KB], turned[:, 2:4, 0:KB]))
            set_wait(act, "pe", "logits")
            copy(resA[:, E:RES], ps[0:KA, 3, 0:NE])
            given("act", "logits", copy(resB[:, E:RES], ps[0:KB, 3, NE:2 * NE]))
            set_wait(act, "pe", "values")
            given("act", "values", copy(wv3[:, :, 0:HD], ps[0:U, 4, 0:E].rearrange("p (h d) -> p h d", h=HEADS)))
            set_wait(act, "pe", "qk")
            given("act", "qk", copy(qk[:].rearrange("p a h u -> p (a h u)"), ps[0:HD, 5, 0:2 * HEADS * U]))
            set_wait(act, "pe", "bmat")
            given("act", "bmat", copy(bmat[:].rearrange("p (a b) f -> p a (b f)", b=2), ps[0:U, 0:6, 0:4 * NF]))
            for h in range(HEADS):
                set_wait(act, "pe", f"factors{h}")
                if h >= 2:
                    set_wait(act, "dve", f"score{h - 2}")
                given("act", f"factors{h}", copy(afac[:, h % 2], factors(h)[:, 1]))

            def S1(s):
                act.wait_ge(s_psum1, s + 1)
                copy(pT[:].rearrange("p i j -> p j i"),
                     ps[:, 0, 0:NTOK].rearrange("p (j i) -> p j i", j=G)).then_inc(s_pT, 1)

            def S3(s):
                act.wait_ge(s_g, s + 1)
                copy(gts[:].rearrange("p i f -> p (i f)"), ps[0:U, 0, 0:IPS * NF]).then_inc(s_gts, 1)
                act.wait_ge(s_phT, s + 1)
                copy(phiT[:].rearrange("p (a b) -> p a b", a=2), ps[0:NF, 1:3, 0:IPS * TOK]).then_inc(s_phTs, 1)

            def S5(s):
                act.wait_ge(s_u, s + 1)
                hh = HEADS // 2
                w = hh * IPS * HV
                copy(us[:, 0:hh].rearrange("p h i v -> p (h i v)"), ps[0:NF, 2, 0:w])
                copy(us[:, hh:HEADS].rearrange("p h i v -> p (h i v)"), ps[0:NF, 0, 0:w]).then_inc(s_us, 1)

            def S7(s):
                for g in range(2):
                    act.wait_ge(s_turn, s * 4 + 2 * g + 1)
                    copy(attA[:, g * IPS * TOK:(g + 1) * IPS * TOK],
                         ps[0:KA, TURN[2 * g], 0:IPS * TOK]).then_inc(s_tA, 1)

            def S8(s):
                act.wait_ge(s_stored, s + 1)
                for q in range(4):
                    act.wait_ge(s_res, s * 4 + q + 1)
                    copy(h1s[:, 2 * q:2 * q + 2, :],
                         ps[0:TOK, RESB[q], 0:2 * RES].rearrange("p (a r) -> p a r", a=2)).then_inc(s_h1, 1)

            def R(s):
                act.wait_ge(s_gap, s + 1)
                nc.scalar.activation(th[:], gap[:], ACT.Tanh, scale=0.5).then_inc(s_th, 1)

            def M(j, b, m):
                act.wait_ge(s_h, j * MC + m + 1)
                nc.scalar.activation(hT[:, m, :], ps[:, HB[m], :], ACT.Gelu,
                                     bias=b1s[:, b, m:m + 1]).then_inc(s_hT, 1)

            def X(j, b):
                act.wait_ge(s_xt, j * 2 + 3)
                copy(xT[:, 0, :], ps[0:KH, XB[0], :]).then_inc(s_xa, 1)

            def N(j, b, n):
                if n % 2 == 0:
                    return
                act.wait_ge(s_y, j * TP + n + 1)
                if n == 1:
                    act.wait_ge(s_gate, j + 1)
                for i in (n - 1, n):
                    nc.scalar.activation(ys[:, b, i, :], yout(i), ACT.Copy,
                                         scale=gate[:, b, i:i + 1]).then_inc(s_ys, 1)

            schedule(act, {"S1": S1, "S3": S3, "S5": S5, "S7": S7, "S8": S8, "R": R, "M": M, "X": X, "N": N},
                     prime=lambda: X(-1, -1))

        @block.tensor
        def _(pe):
            mm = nc.tensor.matmul
            ident = const("ident")

            def turn(dst, src):
                n = src.shape[0]
                return nc.tensor.transpose(dst, src, ident[0:n, 0:n])

            set_wait(pe, "dve", "router")
            for hf in range(2):
                cols = slice(hf * KH, (hf + 1) * KH)
                turn(ps[0:KH, 0, hf * C:(hf + 1) * C], cwc[:, cols])
                turn(ps[0:KH, 0, 64 + hf * NE:64 + (hf + 1) * NE], rts[:, cols])
                turn(ps[0:KH, 1, hf * KA:hf * KA + KA], resA[:, cols])
                last = turn(ps[0:KH, 1, (2 + hf) * KA:(2 + hf) * KA + KB], resB[:, cols])
            given("pe", "turned", last)
            set_wait(pe, "pool", "fills")
            set_wait(pe, "dve", "cwT")
            for i in range(IPS):
                for hf in range(2):
                    last = mm(ps[CPAD * i:CPAD * i + C, 2, 0:C], cwT[:, hf, 1:U], cwT[:, hf, 1:U],
                              start=hf == 0, stop=hf == 1)
            given("pe", "gram", last)
            set_wait(pe, "dve", "rtT")
            set_wait(pe, "act", "resT")
            for r, k in ((0, KA), (1, KB)):
                for hf in range(2):
                    last = mm(ps[0:k, 3, r * NE:(r + 1) * NE], resT[:, 2 * r + hf, 0:k], rtT[:, hf, :],
                              start=hf == 0, stop=hf == 1)
            given("pe", "logits", last)
            for hf in range(2):
                last = mm(ps[0:U, 4, 0:E], cwT[:, hf, :], wqkv[:, hf, 2 * E:3 * E], start=hf == 0, stop=hf == 1)
            given("pe", "values", last)
            for a in range(2):
                for h in range(HEADS):
                    o = (a * HEADS + h) * U
                    for hf in range(2):
                        last = mm(ps[0:HD, 5, o:o + U], wqkv[:, hf, a * E + h * HD:a * E + (h + 1) * HD],
                                  cwT[:, hf, :], start=hf == 0, stop=hf == 1)
            given("pe", "qk", last)
            set_wait(pe, "act", "qk")
            for h in range(HEADS):
                last = mm(ps[0:U, 6, h * U:(h + 1) * U], qk[:, 0, h, :], qk[:, 1, h, :], start=True, stop=True)
            given("pe", "amat", last)
            set_wait(pe, "dve", "amat")
            for h in range(HEADS):
                last = mm(ps[0:U, h // 2, (h % 2) * 2 * NF:(h % 2 + 1) * 2 * NF], amat[:, h, :],
                          const("self", U), start=True, stop=True)
            given("pe", "bmat", last)
            set_wait(pe, "act", "bmat")
            selg = const("selg", U)
            for h in range(HEADS):
                if h >= 6:
                    set_wait(pe, "dve", f"score{h - 6}")
                for k in range(4):
                    last = mm(ps[0:NF, h % 6, k * NF:(k + 1) * NF], selg[:, k * NF:(k + 1) * NF],
                              bmat[:, h, (k % 2) * NF:(k % 2 + 1) * NF], start=True, stop=True)
                given("pe", f"factors{h}", last)
            set_wait(pe, "dve", "b2")

            def S1(s):
                pe.wait_ge(s_pooled, s * CHUNKS + CHUNKS)
                lhs = red[:].rearrange("p i c j -> p (i c) j")
                for jj in range(G):
                    last = mm(ps[:, 0, jj * G:(jj + 1) * G], lhs[:, :, jj], const("rowsel", ROWP),
                              start=True, stop=True)
                last.then_inc(s_psum1, 1)

            def S2(s):
                pe.wait_ge(s_pT, s + 1)
                for hf in range(2):
                    last = mm(ps[0:TOK, 1, hf * 96:(hf + 1) * 96],
                              pT[:, hf * G // 2:(hf + 1) * G // 2, :].rearrange("p i j -> p (i j)"), mix,
                              start=True, stop=True)
                last.then_inc(s_mix, 1)

            def S3(s):
                pe.wait_ge(s_phi, s + 1)
                for i in range(IPS):
                    for hf in range(2):
                        t = hf * IPS + i
                        last = mm(ps[0:U, 0, i * NF:(i + 1) * NF], phi[:, t, 0:U], phi[:, t, :],
                                  start=hf == 0, stop=hf == 1)
                last.then_inc(s_g, 1)
                for t in range(NT):
                    last = turn(ps[0:NF, 1 + t // IPS, (t % IPS) * TOK:(t % IPS + 1) * TOK], phi[:, t, :])
                last.then_inc(s_phT, 1)

            def S4(s):
                pe.wait_ge(s_gts, s + 1)
                pe.wait_ge(s_phTs, s + 1)
                for i in range(IPS):
                    last = mm(ps[0:NF, i // 2, (i % 2) * NV:(i % 2 + 1) * NV], gts[:, i, :],
                              const("wvinit", U), start=True, stop=True)
                last.then_inc(s_gw, 1)

            def S5(s):
                pe.wait_ge(s_gws, s + 1)
                for h in range(HEADS):
                    w = IPS * HV
                    bank, o = (2, h) if h < HEADS // 2 else (0, h - HEADS // 2)
                    last = mm(ps[0:NF, bank, o * w:(o + 1) * w].rearrange("p (i v) -> p i v", i=IPS),
                              score[:, h, :], gws[:, :, h * HV:(h + 1) * HV], start=True, stop=True)
                last.then_inc(s_u, 1)

            def S6(s):
                pe.wait_ge(s_us, s + 1)
                for t in range(NT):
                    q = t // 2
                    if t == 6:
                        pe.wait_ge(s_att, s * 4 + 1)
                    last = mm(ps[0:TOK, NUMB[q], (t % 2) * NV:(t % 2 + 1) * NV],
                              phiT[:, t * TOK:(t + 1) * TOK], us[:, :, t % IPS, :], start=True, stop=True)
                    if t % 2:
                        last.then_inc(s_num, 1)

            def S7(s):
                for g in range(2):
                    for c in range(2):
                        k, w, o = 2 * g + c, (KA, KB)[c], (0, KA)[c]
                        pe.wait_ge(s_att, s * 4 + (2, 3, 4, 4)[k])
                        if k == 3:
                            pe.wait_ge(s_tA, s * 2 + 1)
                        for i in range(IPS):
                            last = turn(ps[0:w, TURN[k], i * TOK:(i + 1) * TOK], att[:, g * IPS + i, o:o + w])
                        last.then_inc(s_turn, 1)

            def S8(s):
                for q in range(4):
                    pe.wait_ge(s_tA, s * 2 + (1, 2, 2, 2)[q])
                    pe.wait_ge(s_tB, s * 2 + (1, 1, 2, 2)[q])
                    if q == 3:
                        pe.wait_ge(s_h1, s * 4 + 1)
                    for t in (2 * q, 2 * q + 1):
                        o = ps[0:TOK, RESB[q], (t % 2) * RES:(t % 2 + 1) * RES]
                        mm(o, attA[:, t * TOK:(t + 1) * TOK], resA[:], start=True, stop=False)
                        last = mm(o, attB[:, t * TOK:(t + 1) * TOK], resB[:], start=False, stop=True)
                    last.then_inc(s_res, 1)

            def S9(s):
                pe.wait_ge(s_mask, s + 1)
                w = (NT + 1) * NE
                mm(ps[:, 1, 0:w], tri[:], mask[:], start=True, stop=False)
                for k in range(1, NT + 1):
                    last = mm(ps[:, 1, k * NE:w], ones[:], mask[:, 0:w - k * NE], start=False, stop=k == NT)
                last.then_inc(s_rank, 1)

            def M(j, b, m):
                if m == 0:
                    pe.wait_ge(d_tile[b], tile_landed(j, b))
                    pe.wait_ge(s_xa, j + 1)
                    pe.wait_ge(s_xd, j + 1)
                elif m >= 3:
                    pe.wait_ge(s_hT, j * MC + m - 2)
                for hf in range(2):
                    last = mm(ps[:, HB[m], :], w1s[:, b, hf, m * 128:(m + 1) * 128], xT[:, hf, :],
                              start=hf == 0, stop=hf == 1)
                last.then_inc(s_h, 1)

            def X(j, b, first=False):
                nb = (b + 1) % 3
                pe.wait_ge(d_tile[nb], tile_landed(j + 1, nb))
                for hf in range(2):
                    if not first:
                        pe.wait_ge(s_hT, j * MC + 4 + hf)
                    for n in range(TP):
                        last = turn(ps[0:KH, XB[hf], n * 128:(n + 1) * 128], xr[:, nb, n, hf * KH:(hf + 1) * KH])
                    last.then_inc(s_xt, 1)

            def N(j, b, n):
                if n == 0:
                    pe.wait_ge(s_hT, j * MC + MC)
                for m in range(MC):
                    mm(yout(n), hT[:, m, n * 128:(n + 1) * 128], w2s[:, b, m, :], start=m == 0, stop=False)
                mm(yout(n), ones[0:3, :], b2t[:, b, :], start=False, stop=True).then_inc(s_y, 1)

            schedule(pe, {"S1": S1, "S2": S2, "S3": S3, "S4": S4, "S5": S5, "S6": S6, "S7": S7, "S8": S8,
                          "S9": S9, "M": M, "X": X, "N": N}, prime=lambda: X(-1, -1, first=True))

        @block.vector
        def _(dve):
            V = nc.vector
            step_links, tile_links = 21, 10
            pos_ = {"step": 0, "tile": 0}

            def mark(ins, kind="step"):
                pos_[kind] += 1
                return ins.then_inc(s_dve if kind == "step" else s_dvt, 1)

            def own(i, kind="step", alone=False):
                wait = wait_first if alone else type(dve).wait_ge
                if kind == "step":
                    wait(dve, s_dve, i * step_links + pos_["step"])
                else:
                    wait(dve, s_dvt, i * tile_links + pos_["tile"])

            def bc(ap, n):
                return ap.unsqueeze(len(ap.shape)).to_broadcast(list(ap.shape) + [n])

            def P(s, k):
                s1 = s + 1
                dve.wait_ge(d_x[k % XSLOTS], s1 * (16 * CHUNKS // XSLOTS) + 16 * (k // XSLOTS) + 16)
                n = CH // 2
                for c in (0, n):
                    o = CH * (k % 2) + c
                    last = V.tensor_reduce(red[:, k // 2, o:o + n, :],
                                           xbuf[:, k % XSLOTS, c:c + n, :]
                                           .rearrange("p c (r j w) -> p c j r w", r=2, j=G), AX.XY, ALU.add)
                last.then_inc(s_pooled, 1)

            n_set = [0]

            def link(ins):
                n_set[0] += 1
                ins.then_inc(s_dvs, 1)
                dve.wait_ge(s_dvs, n_set[0])

            dve.wait_ge(d_cst, 16)
            V.tensor_copy(base[:], const("base"))
            V.tensor_copy(cons[:], const("base"))
            V.tensor_copy(ids[:], const("ids", TOK))
            given("dve", "copies", V.tensor_copy(tri[:], const("tri", TOK)))
            dve.wait_ge(d_w, 16 * 9)
            link(V.tensor_reduce(small[:, 0:1], cws[:], AX.X, ALU.add))
            link(V.tensor_scalar(small[:, 1:2], small[:, 0:1], -1.0 / E, None, ALU.mult))
            given("dve", "cwc", V.tensor_scalar(cwc[:], cws[:], small[:, 1:2], None, ALU.add))
            link(V.tensor_reduce(smallr[:, 0:1], rts[:], AX.X, ALU.add))
            link(V.tensor_scalar(smallr[:, 1:2], smallr[:, 0:1], -1.0 / E, None, ALU.mult))
            given("dve", "router", V.tensor_scalar(rts[:], rts[:], smallr[:, 1:2], None, ALU.add))
            set_wait(dve, "pe", "turned")
            given("dve", "cwT", V.tensor_copy(cwT[:, :, 1:U], ps[0:KH, 0, 0:2 * C].rearrange("p (a c) -> p a c", a=2)))
            given("dve", "rtT", V.tensor_copy(rtT[:], ps[0:KH, 0, 64:64 + 2 * NE].rearrange("p (a c) -> p a c", a=2)))
            set_wait(dve, "pe", "gram")
            for i in range(IPS):
                o = IPS * C + i * C
                last = V.tensor_scalar(mix[CPAD * i:CPAD * i + C, o:o + C], ps[CPAD * i:CPAD * i + C, 2, 0:C],
                                       1.0 / E, None, ALU.mult)
            given("dve", "mix", last)
            set_wait(dve, "pe", "amat")
            given("dve", "amat", V.scalar_tensor_tensor(
                out=amat[:], in0=ps[0:U, 6, 0:HEADS * U].rearrange("p (h u) -> p h u", h=HEADS), scalar=HD ** -0.5,
                in1=const("e00", U).unsqueeze(1).to_broadcast([U, HEADS, U]), op0=ALU.mult, op1=ALU.add))
            set_wait(dve, "pool", "fills")
            for h in range(HEADS):
                if h < CHUNKS:
                    P(-1, h)
                set_wait(dve, "act", f"factors{h}")
                if h:
                    set_wait(dve, "dve", f"score{h - 1}")
                link(V.tensor_tensor(atmp[:], factors(h)[:, 0], afac[:, h % 2], ALU.mult))
                given("dve", f"score{h}", V.tensor_tensor(score[:, h, :], atmp[:, 0], atmp[:, 1], ALU.add))
            set_wait(dve, "dve", f"score{HEADS - 1}")
            given("dve", "score", V.tensor_scalar(score[0:1, :, 0:1], score[0:1, :, 0:1], 0.5, None, ALU.add))
            link(V.tensor_copy(b2s[:, 0], b2f[:, 0]))
            link(V.tensor_tensor(b2f[:, 1], b2f[:, 0], b2s[:, 0], ALU.subtract))
            link(V.tensor_copy(b2s[:, 1], b2f[:, 1]))
            link(V.tensor_tensor(b2f[:, 0], b2f[:, 1], b2s[:, 1], ALU.subtract))
            given("dve", "b2", V.tensor_copy(b2s[:, 2], b2f[:, 0]))

            att_ch = att[:, :, E:E + C]

            def S2(s):
                pos_["step"] = 0
                dve.wait_ge(s_mix, s + 1)
                mixed = ps[0:TOK, 1, 0:192].rearrange("p (a b c) -> p a b c", a=2, b=2 * IPS)
                att4 = att_ch.rearrange("p (a b) c -> p a b c", a=2)
                mark(V.tensor_copy(att4, mixed[:, :, 0:IPS]))
                own(s)
                mark(V.tensor_tensor(prod[:].rearrange("p (a b) c -> p a b c", a=2), att4, mixed[:, :, IPS:2 * IPS],
                                     ALU.mult))
                own(s)
                mark(V.tensor_reduce(var1[:], prod[:], AX.X, ALU.add))
                own(s)
                V.tensor_scalar(var1[:], var1[:], EPS, None, ALU.add).then_inc(s_var1, 1)
                dve.wait_ge(s_rstd1, s + 1)
                mark(V.tensor_tensor(phi[:, :, 1:U], att_ch, bc(rstd1[:], C), ALU.mult))
                own(s)
                for i in range(1, U):
                    last = V.tensor_tensor(phi[:, :, FOFF[i]:FOFF[i] + U - i], phi[:, :, i:U],
                                           phi[:, :, i:i + 1].to_broadcast([TOK, NT, U - i]), ALU.mult)
                last.then_inc(s_phi, 1)

            def S4(s):
                dve.wait_ge(s_gw, s + 1)
                V.tensor_copy(gws[:].rearrange("p (a b) v -> p a (b v)", a=2), ps[0:NF, 0:2, 0:2 * NV]).then_inc(s_gws, 1)

            def S6(s):
                for q in range(4):
                    dve.wait_ge(s_num, s * 4 + q + 1)
                    num = ps[0:TOK, NUMB[q], 0:2 * NV].rearrange("p (a h v) -> p a h v", a=2, h=HEADS)
                    if q:
                        dve.wait_ge(s_att, s * 4 + q)
                    mark(V.reciprocal(rden[:].unsqueeze(3), num[:, :, :, HD:HV]))
                    own(s)
                    V.tensor_tensor(att[:, 2 * q:2 * q + 2, 0:E].rearrange("p a (h d) -> p a h d", h=HEADS),
                                    num[:, :, :, 0:HD], bc(rden[:], HD), ALU.mult).then_inc(s_att, 1)

            def S7(s):
                for g in range(2):
                    dve.wait_ge(s_turn, s * 4 + 2 * g + 2)
                    V.tensor_copy(attB[:, g * IPS * TOK:(g + 1) * IPS * TOK],
                                  ps[0:KB, TURN[2 * g + 1], 0:IPS * TOK]).then_inc(s_tB, 1)

            def S8(s):
                for q in range(4):
                    dve.wait_ge(s_h1, s * 4 + q + 1)
                    for t in (2 * q, 2 * q + 1):
                        V.bn_stats(stats[:, t, :], h1s[:, t, 0:E])
                        last = V.max(top[:, t, :], h1s[:, t, E:RES])
                mark(last)
                own(s, alone=True)
                for t in range(NT):
                    V.bn_aggr(mv[:, t, :], stats[:, t, :])
                    last = V.max_index(topi[:, t, :], top[:, t, :], h1s[:, t, E:RES])
                mark(last)
                own(s, alone=True)
                V.tensor_scalar(var2[:].unsqueeze(2), mv[:, :, 1:2], EPS, None, ALU.add).then_inc(s_var2, 1)
                V.tensor_tensor(gap[:].unsqueeze(2), top[:, :, 0:1], top[:, :, 1:2], ALU.subtract)
                mark(V.tensor_copy(idxf[:].rearrange("p k t -> p t k"), topi[:, :, 0:2]))
                own(s)
                mark(V.tensor_tensor(hot[:], bc(idxf[:].rearrange("p k t -> p (k t)"), NE),
                                     const("iota", TOK).unsqueeze(1).to_broadcast([TOK, 2 * NT, NE]), ALU.is_equal))
                own(s)
                V.tensor_tensor(mask[:, 0:NT * NE].rearrange("p (t e) -> p t e", t=NT), hot[:, 0:NT, :],
                                hot[:, NT:2 * NT, :], ALU.add).then_inc(s_mask, 1)

            def R(s):
                dve.wait_ge(s_rstd2, s + 1)
                V.tensor_tensor(gap[:], gap[:], rstd2[:], ALU.mult).then_inc(s_gap, 1)
                dve.wait_ge(s_listed, s + 1)
                for t in range(NT):
                    V.tensor_scalar(rows[:, t, 0:E], h1s[:, t, 0:E], mv[:, t, 0:1], rstd2[:, t:t + 1],
                                    ALU.subtract, ALU.mult)
                mark(V.tensor_copy(rows[:, :, ROW - 1:ROW].bitcast(I32), ids[:].unsqueeze(2)))
                own(s)
                mark(V.tensor_scalar(ids[:], ids[:], float(IPS * NTOK), None, ALU.add))
                dve.wait_ge(s_th, s + 1)
                V.tensor_scalar(gk[:, 0], th[:], 0.5, 0.5, ALU.mult, ALU.add)
                mark(V.tensor_scalar(gk[:, 1], th[:], -0.5, 0.5, ALU.mult, ALU.add))
                own(s)
                mark(V.tensor_tensor(hotw[:], hot[:], bc(gk[:].rearrange("p k t -> p (k t)"), NE), ALU.mult))
                own(s)
                mark(V.tensor_tensor(rows[:, :, E:E + NE], hotw[:, 0:NT, :], hotw[:, NT:2 * NT, :], ALU.add))

            def S9(s):
                dve.wait_ge(s_rank, s + 1)
                own(s)
                mark(V.tensor_tensor(pos[:].rearrange("p (t e) -> p t e", t=NT),
                                ps[0:TOK, 1, 0:NT * NE].rearrange("p (t e) -> p t e", t=NT),
                                base[0:TOK].unsqueeze(1).to_broadcast([TOK, NT, NE]), ALU.add))
                own(s)
                mark(V.tensor_tensor(base[:], ps[:, 1, NT * NE:(NT + 1) * NE], base[:], ALU.add))
                own(s)
                mark(V.tensor_tensor(hotw[:].rearrange("p (k t) e -> p k (t e)", k=2),
                                     hot[:].rearrange("p (k t) e -> p k (t e)", k=2),
                                     pos[:].unsqueeze(1).to_broadcast([TOK, 2, NT * NE]), ALU.mult))
                own(s)
                mark(V.tensor_reduce(slotf[:], hotw[:], AX.X, ALU.add))
                own(s)
                V.tensor_copy(sloti[:], slotf[:]).then_inc(s_slots, 1)
                assert pos_["step"] == step_links, pos_

            def L(j, b, first=False):
                nb = (b + 1) % 3
                i = j + 1
                pos_["tile"] = 0

                def then(ins, alone=False):
                    mark(ins, "tile")
                    own(i, "tile", alone)

                then(V.tensor_tensor(pend[:], base[:], cons[:], ALU.subtract), alone=True)
                then(V.max(pmax[:], pend[:]), alone=True)
                then(V.max_index(pidx[:], pmax[:], pend[:]))
                V.tensor_copy(pick[:, 0:1], pidx[:, 0:1])
                then(V.tensor_scalar(pick[:, 1:2], pmax[:, 0:1], 0.0, None, ALU.is_le))
                then(V.tensor_scalar(hotE[:, nb], const("iota"), pick[:, 0:1], None, ALU.is_equal))
                then(V.tensor_tensor(tmpE[:], hotE[:, nb], cons[:], ALU.mult))
                V.tensor_reduce(pick[:, 2:3], tmpE[:], AX.X, ALU.add)
                then(V.scalar_tensor_tensor(out=cons[:], in0=hotE[:, nb], scalar=float(T), in1=cons[:],
                                            op0=ALU.mult, op1=ALU.add))
                then(V.tensor_scalar(pick[:, 3:4], pick[:, 2:3], -1.0, float(IDLE), ALU.mult, ALU.add))
                then(V.scalar_tensor_tensor(out=pick[:, 4:5], in0=pick[:, 3:4], scalar=pick[:, 1:2],
                                            in1=pick[:, 2:3], op0=ALU.mult, op1=ALU.add))
                if not first:
                    dve.wait_ge(s_picked, i)
                V.tensor_copy(seli[0:1, 0:1], pick[0:1, 0:1])
                V.tensor_copy(seli[0:1, 1:2], pick[0:1, 4:5]).then_inc(s_pick, 1)

            def X(j, b, first=False):
                nb = (b + 1) % 3
                dve.wait_ge(d_tile[nb], tile_landed(j + 1, nb))
                if not first:
                    dve.wait_ge(s_gate, j + 1)
                mark(V.tensor_tensor(gmul[:], xr[:, nb, :, E:E + NE],
                                     hotE[:, nb].unsqueeze(1).to_broadcast([128, TP, NE]), ALU.mult), "tile")
                own(j + 1, "tile")
                V.tensor_reduce(gate[:, nb], gmul[:], AX.X, ALU.add).then_inc(s_gate, 1)
                assert pos_["tile"] == tile_links, pos_
                dve.wait_ge(s_xt, j * 2 + 4)
                V.tensor_copy(xT[:, 1, :], ps[0:KH, XB[1], :]).then_inc(s_xd, 1)

            def prime():
                L(-1, -1, first=True)
                X(-1, -1, first=True)

            def list_ends():
                V.tensor_copy(endi[:], base[0:1, :]).then_inc(s_ends, 1)

            schedule(dve, {"P": P, "S2": S2, "S4": S4, "S6": S6, "S7": S7, "S8": S8, "R": R, "S9": S9, "L": L, "X": X},
                     prime=prime, before_tail=list_ends)
    return nc


_INS = ["x", "L0_tok_channel_weights", "L0_attn_w_qkv", "L0_attn_w_proj", "L0_attn_b_proj", "L0_ffn_router_w",
        "L0_ffn_w1", "L0_ffn_b1", "L0_ffn_w2", "L0_ffn_b2"]


def kernel(**inputs):
    import concourse.bacc as bacc
    from concourse.bass_utils import run_bass_kernel_spmd as run

    nc = bacc.Bacc("TRN2", target_bir_lowering=False, num_devices=1)
    arrays, args = {}, []

    def give(name, a):
        arrays[name] = np.ascontiguousarray(a)
        args.append(nc.dram_tensor(name, arrays[name].shape, mybir.dt.from_np(arrays[name].dtype),
                                   kind="ExternalInput").ap())

    for name in _INS:
        a = np.asarray(inputs[name])
        if name == "L0_ffn_b1":
            a = a.reshape(NE, MC, 128).transpose(0, 2, 1)
        give(name, a)
    for name, a in zip(("consts", "padids"), constants()):
        give(name, a)
    args.append(nc.dram_tensor("result", (TOKENS + T, E), F32, kind="ExternalOutput").ap())
    vit_layer(nc, *args)
    got = run(nc, [arrays], core_ids=[0]).results[0]["result"]
    return got[:TOKENS].reshape(B, NTOK, E)
```

```python
from contextlib import ExitStack

import numpy as np

import concourse.bass as bass
from concourse import mybir

ALU = mybir.AluOpType
ACT = mybir.ActivationFunctionType
F32 = mybir.dt.float32
F32R = mybir.dt.float32r
BF16 = mybir.dt.bfloat16
I32 = mybir.dt.int32
U32 = mybir.dt.uint32
AX = mybir.AxisListType

B, C, IMG, PATCH = 64, 12, 224, 16
G = IMG // PATCH
NTOK = G * G
E = 192
HEADS, HD = 12, 16
NE, FF = 8, 768
EPS = 1e-5

IPS = 4
STEPS = B // IPS
TOK = NTOK // 2
NT = 2 * IPS
ROWP = IMG // 2
U = C + 1
NF = U * (U + 1) // 2
FOFF = [sum(U - a for a in range(i)) for i in range(U)]
HV = HD + 1
NV = HEADS * HV
ATT = E + U
KA = (ATT + 1) // 2
KB = ATT - KA
RES = E + NE
ROW = E + NE + 1
T = 512
TP = T // 128
MC = FF // 128
KH = E // 2
KB1 = E - 128
TOKENS = B * NTOK
CAP = TOKENS + T
IDLE = NE * CAP
CHUNKS = 2 * IPS
XSLOTS = 4
CH = C // 2
TILES_PER_STEP = 3
PRO = 4
TILES = 57
TAIL = (TILES - (STEPS - PRO) * TILES_PER_STEP) // TILES_PER_STEP
for _s in range(PRO, STEPS):
    assert 2 * NTOK * IPS * _s - T * (TILES_PER_STEP * (_s - PRO + 1) + 1) > NE * (T - 1)
assert 2 * NTOK * IPS * PRO - T > NE * (T - 1)
assert TILES * T > 2 * TOKENS + NE * (T - 1)

_C = {}
_W = 0
for _n, _w in (("ident", 128), ("rowsel", G), ("mixinit", 2 * IPS * C), ("spread", IPS * C), ("block", IPS * C),
               ("self", 2 * NF), ("selg", 4 * NF),
               ("e00", U), ("half", NF), ("wvinit", NV), ("iota", NE), ("base", NE), ("ids", NT),
               ("tri", 128)):
    _C[_n] = (_W, _w)
    _W += _w
CONSTS = _W


def constants():
    c = np.zeros((128, CONSTS), np.float32)

    def put(name, a, rows):
        o, w = _C[name]
        c[:rows, o:o + w] = np.asarray(a, np.float32).reshape(rows, w)

    put("ident", np.eye(128), 128)
    put("rowsel", np.arange(ROWP)[:, None] // (PATCH // 2) == np.arange(G), ROWP)
    w = IPS * C
    put("mixinit", np.eye(w, 2 * w), w)
    put("spread", np.tile(np.eye(C), (1, IPS)), C)
    put("block", np.kron(np.eye(IPS), np.ones((C, C))), w)
    first = np.zeros((U, NF))
    second = np.zeros((U, NF))
    once = np.ones(NF)
    for i in range(U):
        for k in range(i, U):
            f = FOFF[i] + k - i
            first[i, f] = second[k, f] = 1
            if i == k:
                once[f] = 0.5
    put("self", np.concatenate([first * once, second], 1), U)
    put("selg", np.concatenate([first * once, second, second * once, first], 1), U)
    e00 = np.zeros((U, U))
    e00[0, 0] = 1
    put("e00", e00, U)
    half = np.zeros((NF, NF))
    half[0, 0] = 0.5
    put("half", half, NF)
    wv = np.zeros((U, HEADS, HV))
    wv[0, :, HD] = 1
    put("wvinit", wv, U)
    put("iota", np.tile(np.arange(NE), (128, 1)), 128)
    put("base", np.tile(np.arange(NE) * CAP, (128, 1)), 128)
    t = np.arange(NT)
    put("ids", (t % IPS) * NTOK + (t // IPS) * TOK + np.arange(TOK)[:, None], TOK)
    put("tri", np.arange(TOK)[:, None] < np.where(np.arange(128) < TOK, np.arange(128), 0), TOK)
    pad = np.arange(TOKENS, TOKENS + T, dtype=np.int32).reshape(128, TP)
    return c, pad


STEP_ALONE = ("S1 S2 S3 S4 " + 21 * "P " + "S5 S6.0 S6.1 S6.2 S6.3 P P P P S7.0 S7.1 P P P P P P S8.0 P S8.1 P S8.2 P S8.3 P S10 "
              "R P P V.0 V.1 V.2 V.3 S11 P P S9 P P P P P P P P P Q0 Q1 Q2 Q3").split()
ORDER = [
    """S1 P P P P M0 P P M1 P Z1 K S2 M2 P P N0 M3 P P W0 X0 P <F N1 P S3 M4 L X1 P P N2 P S4 M5 P W1 J N3 Z0 P P S5
       P""".split(),
    """M0 P S6.0 <N4 P M1 <N5 P <Y Z1 <A S6.1 P K M2 S6.2 P N0 P M3 P S6.3 W0 S7.0 X0 P N1 S7.1 <F P M4 L P S8.0 X1 P P
       N2 S8.1 P M5 P S8.2 W1 J N3 P S8.3 Z0 P P S10""".split(),
    """M0 P <N4 R M1 <N5 P <Y Z1 <A K V.0 S11 M2 P S9 P N0 V.1 M3 V.2 W0 P <F X0 N1 V.3 P M4 Q0 P X1 P N2 Q1 M5 N3 N4 N5
       Y L W1 Z0 Q2 J P P P Q3 A""".split(),
]
PARTS = IPS * C
assert STEP_ALONE.count("P") == sum(o.count("P") for o in ORDER) == PARTS


def vit_layer(nc, x, cw, w_qkv, w_proj, b_proj, router, w1, b1, w2, b2, consts, padids, out):
    rows_d = nc.dram_tensor("rows_d", [IDLE + T, ROW], F32, kind="Internal").ap()
    b2_d = nc.dram_tensor("b2_d", [NE, 3, E], BF16, kind="Internal").ap()

    with ExitStack() as ctx:
        def sb(name, shape, dt=F32):
            return ctx.enter_context(nc.sbuf_tensor(name, shape, dt))

        def sem(name):
            return ctx.enter_context(nc.semaphore(name))

        ps = ctx.enter_context(nc.psum_tensor("ps", [128, 8, 512], F32))

        cst = sb("cst", [128, CONSTS])
        tri = sb("tri", [TOK, 128], BF16)
        ones = sb("ones", [TOK, 128], BF16)
        mix = cst[0:IPS * C, _C["mixinit"][0]:_C["mixinit"][0] + 2 * IPS * C]
        gram = sb("gram", [C, C + IPS * C])
        cws = sb("cws", [C, E])
        cwc = sb("cwc", [C, E])
        cwT = sb("cwT", [KH, 2, U])
        rts = sb("rts", [NE, E])
        rtT = sb("rtT", [KH, 2, NE])
        small = sb("small", [C, 4])
        smallr = sb("smallr", [NE, 4])
        resA = sb("resA", [KA, RES])
        resB = sb("resB", [KB, RES])
        resT = sb("resT", [KH, 4, KA])
        qk = sb("qk", [HD, 2, HEADS, U])
        amat = sb("amat", [U, HEADS, U])
        afac = sb("afac", [NF, 2, 2, NF])
        atmp = sb("atmp", [NF, 2, NF])
        score = sb("score", [NF, HEADS, NF])
        b2f = sb("b2f", [NE, 2, E])
        b2s = sb("b2s", [NE, 3, E], BF16)
        pad = sb("pad", [128, TP, ROW])
        padi = sb("padi", [128, TP], I32)

        xbuf = sb("xbuf", [ROWP, XSLOTS, CH, 2 * IMG])
        red = sb("red", [ROWP, IPS, C, G])
        pT = sb("pT", [IPS * C, G, G])
        prod = sb("prod", [TOK, NT, C])
        var1 = sb("var1", [TOK, NT])
        rstd1 = sb("rstd1", [TOK, NT])
        newton = sb("newton", [TOK, 2, NT])
        phi = sb("phi", [TOK, NT, NF])
        gts = sb("gts", [U, IPS, NF])
        phiT = sb("phiT", [NF, NT * TOK])
        gws = sb("gws", [NF, IPS, NV])
        us = sb("us", [NF, HEADS, IPS, HV])
        rden = sb("rden", [TOK, 2, HEADS])
        att = sb("att", [TOK, NT, ATT])
        attA = sb("attA", [KA, NT * TOK])
        attB = sb("attB", [KB, NT * TOK])
        h1s = sb("h1s", [TOK, NT, RES])
        stats = sb("stats", [TOK, NT, 6])
        mv = sb("mv", [TOK, NT, 2])
        var2 = sb("var2", [TOK, NT])
        rstd2 = sb("rstd2", [TOK, NT])
        shift2 = sb("shift2", [TOK, NT])
        top = sb("top", [TOK, NT, NE])
        topi = sb("topi", [TOK, NT, NE], U32)
        gap = sb("gap", [TOK, NT])
        th = sb("th", [TOK, NT])
        idxf = sb("idxf", [TOK, 2, NT])
        hot = sb("hot", [TOK, 2 * NT, NE])
        hotw = sb("hotw", [TOK, 2 * NT, NE])
        gk = sb("gk", [TOK, 2, NT])
        mask = sb("mask", [TOK, (NT + 1) * NE], BF16)
        ids = sb("ids", [TOK, NT])
        base = sb("base", [128, NE])
        pos = sb("pos", [TOK, NT * NE])
        slotf = sb("slotf", [TOK, 2 * NT])
        sloti = sb("sloti", [TOK, 2 * NT], I32)
        rows = sb("rows", [TOK, NT, ROW])

        endi = sb("endi", [1, NE], I32)
        cons = sb("cons", [128, NE])
        pend = sb("pend", [128, NE])
        pmax = sb("pmax", [128, NE])
        pidx = sb("pidx", [128, NE], U32)
        pick = sb("pick", [128, 8])
        hotE = sb("hotE", [128, 3, NE])
        tmpE = sb("tmpE", [128, NE])
        seli = sb("seli", [1, 3, 2], I32)
        avail = sb("avail", [128, NE])
        xr = sb("xr", [128, 3, TP, ROW])
        w1r = sb("w1r", [128, 2, FF])
        w1h = sb("w1h", [128, 2, FF], F32R)
        w1l = sb("w1l", [128, 2, FF], F32R)
        w2r = sb("w2r", [128, MC, E])
        w2h = sb("w2h", [128, MC, E], F32R)
        w2l = sb("w2l", [128, MC, E], F32R)
        b1s = sb("b1s", [128, 3, MC])
        b2t = sb("b2t", [3, 3, E], BF16)
        xh = sb("xh", [128, 3, T], F32R)
        xl = sb("xl", [128, 3, T], F32R)
        xb = sb("xb", [128, 3, T], F32R)
        hf = sb("hf", [128, 2, T])
        hh = sb("hh", [128, 3, T], F32R)
        hl = sb("hl", [128, 3, T], F32R)
        gmul = sb("gmul", [128, TP, NE])
        gate = sb("gate", [128, 3, TP])
        ys = sb("ys", [128, 3, TP, E])
        bmat = ys[0:U].rearrange("p a n e -> p (a n e)")[:, 0:HEADS * 2 * NF].rearrange("p (h f) -> p h f", h=HEADS)
        wqkv = w1r[0:KH].rearrange("p a f -> p (a f)")[:, 0:2 * 3 * E].rearrange("p (a f) -> p a f", a=2)

        def const(name, rows=128):
            o, w = _C[name]
            return cst[0:rows, o:o + w]

        d_cst, d_w, d_b2, d_pad = sem("d_cst"), sem("d_w"), sem("d_b2"), sem("d_pad")
        d_x = [sem(f"d_x{i}") for i in range(XSLOTS)]
        d_h1, d_scat, d_add = sem("d_h1"), sem("d_scat"), sem("d_add")
        d_rows = [sem(f"d_rows{i}") for i in range(3)]
        d_w1, d_w2 = sem("d_w1"), sem("d_w2")
        SETUP = {
            "pool": ["zeros", "fills", "pad"],
            "dve": ["copies", "cwc", "router", "cwT", "rtT", "gram", "wide", "mix", "amat"]
                   + [f"score{h}" for h in range(HEADS)] + ["score", "b2"],
            "act": ["resT", "logits", "values", "qk", "bmat"] + [f"factors{h}" for h in range(HEADS)],
            "pe": ["turned", "gram", "wide", "blocks", "logits", "values", "qk", "amat", "bmat"]
                  + [f"factors{h}" for h in range(HEADS)],
        }
        s_set = {e: sem(f"set_{e}") for e in SETUP}

        def given(engine, name, ins):
            ins.then_inc(s_set[engine], 1)

        def set_wait(eng, engine, name):
            eng.wait_ge(s_set[engine], SETUP[engine].index(name) + 1)

        s_dve = sem("dve_step")
        s_dvs = sem("dve_setup")
        s_dvp = sem("dve_pick")
        s_dvg = sem("dve_gate")
        s_pooled = sem("pooled")
        s_psum1 = sem("rows_summed")
        s_pT = sem("pT_ready")
        s_mix = sem("mix_ready")
        s_phi = sem("phi_ready")
        s_g, s_phT = sem("moments_ready"), sem("phiT_turned")
        s_gts, s_phTs = sem("moments_copied"), sem("phiT_copied")
        s_gw, s_gws = sem("gw_ready"), sem("gw_copied")
        s_u, s_us = sem("u_ready"), sem("u_copied")
        s_num, s_att = sem("num_ready"), sem("att_ready")
        s_turn, s_tA, s_tB = sem("att_turned"), sem("attT_by_act"), sem("attT_by_dve")
        s_res, s_h1 = sem("residual_ready"), sem("residual_copied")
        s_stored = sem("residual_stored")
        s_gap, s_th, s_norm = sem("gap_ready"), sem("tanh_ready"), sem("rows_normalised")
        s_mask, s_rank = sem("mask_ready"), sem("rank_ready")
        s_slots = sem("slots_ready")
        s_listed = sem("rows_listed")
        s_pick = sem("tile_picked")
        s_free = sem("tile_buffers_free")
        s_xt, s_xa, s_xd = sem("rows_turned"), sem("xT_by_act"), sem("xT_by_dve")
        s_w1h, s_w1l = sem("w1_high_ready"), sem("w1_low_ready")
        s_w2h, s_w2l = sem("w2_high_ready"), sem("w2_low_ready")
        s_h, s_hT, s_hl = sem("hidden_ready"), sem("hidden_gelu"), sem("hidden_low_ready")
        s_n, s_y, s_ys = sem("chunk_added"), sem("y_ready"), sem("y_scaled")
        s_gate = sem("gate_ready")
        s_avail = sem("lists_counted")
        s_waits = sem("waits_passed")
        s_ends = sem("list_ends_ready")

        NUMB, TURN, RESB = (1, 2, 0, 1), (2, 0, 1, 2), (0, 1, 2, 0)
        HB, XB = (3, 4, 5, 3, 5, 4), (4, 3)

        def yout(n):
            return ps[:, 6 + n // 2, (n % 2) * E:(n % 2 + 1) * E]

        def factors(h):
            return ps[0:NF, h % 6, 0:4 * NF].rearrange("p (a b f) -> p b a f", a=2, b=2)

        def tile_landed(j, buf):
            return (j - buf) * 16 + 48

        wv3 = const("wvinit", U).rearrange("p (h v) -> p h v", h=HEADS)

        xv = x.rearrange("b c (p r) w -> b p c (r w)", r=2)
        outv = out[0:TOKENS].rearrange("(b h p) e -> b p h e", h=2, p=TOK)

        def tiles_do(eng, handlers, s=None, j=None, with_tiles=True, with_step=True, pooling=True):
            part = 0
            for b, names in enumerate(ORDER if with_tiles else [STEP_ALONE]):
                for name in names:
                    before = name[0] == "<"
                    if name[before] in "LJZKMWXNYAF":
                        if with_tiles and name[before] in handlers:
                            handlers[name[before]](j + b - before, b - before,
                                                   *([int(name[before + 1:])] if name[before + 1:] else []))
                    elif name[0] == "P":
                        if with_step and pooling and "P" in handlers:
                            handlers["P"](s, part)
                        part += 1
                    elif with_step:
                        stage, quarter = (name.split(".") + [""])[0:2] if name[0] != "Q" else ("Q", name[1:])
                        if stage in handlers:
                            handlers[stage](s, *([int(quarter)] if quarter else []))

        def schedule(eng, handlers, prime=None, before_tail=None):
            with eng.Fori(0, PRO) as s:
                tiles_do(eng, handlers, s=s, with_tiles=False)
            if prime:
                prime()
            with eng.Fori(PRO, STEPS - 1) as s:
                tiles_do(eng, handlers, s=s, j=(s - PRO) * TILES_PER_STEP)
            s = STEPS - 1
            tiles_do(eng, handlers, s=s, j=(s - PRO) * TILES_PER_STEP, pooling=False)
            if before_tail:
                before_tail()
            with eng.Fori(0, TAIL) as i:
                tiles_do(eng, handlers, j=i * TILES_PER_STEP + (STEPS - PRO) * TILES_PER_STEP, with_step=False)

        def wait_first(eng, signal, value):
            eng.wait_ge(signal, value)
            eng.sem_inc(s_waits, 1)

        block = ctx.enter_context(nc.Block())

        @block.sync
        def _(sp):
            sp.dma_start(cst[:], consts).then_inc(d_cst, 16)

            def load_chunk(s, k):
                sp.dma_start(xbuf[:, k % XSLOTS],
                             xv[bass.ds(s * IPS + k // 2, 1), :, CH * (k % 2):CH * (k % 2) + CH]
                             .rearrange("b p c w -> p (b c) w")).then_inc(d_x[k % XSLOTS], 16)

            weights = [
                (cws[:], cw), (wqkv, w_qkv.rearrange("(h p) f -> p h f", p=KH)), (rts[:], router),
                (resA[:, 0:E], w_proj[0:KA]), (resB[0:E - KA, 0:E], w_proj[KA:E]),
                (resB[E - KA:E - KA + C, 0:E], cw),
                (resB[E - KA + C:KB, 0:E], b_proj.rearrange("(a e) -> a e", a=1)),
                (b2f[:, 0, :], b2), (padi[:], padids),
            ]
            for dst, src in weights:
                sp.dma_start(dst, src).then_inc(d_w, 16)
            for k in range(XSLOTS):
                load_chunk(0, k)
            for k in range(CHUNKS):
                sp.wait_ge(s_pooled, CH * (k + 1))
                load_chunk((k + XSLOTS) // CHUNKS, (k + XSLOTS) % CHUNKS)

            set_wait(sp, "pool", "pad")
            sp.dma_start(rows_d[IDLE:IDLE + T].rearrange("(p n) c -> p n c", n=TP), pad[:]).then_inc(d_pad, 16)
            sp.dma_start(out[TOKENS:TOKENS + T].rearrange("(p n) c -> p n c", n=TP),
                         pad[:, :, 0:E]).then_inc(d_pad, 16)
            set_wait(sp, "dve", "b2")
            sp.dma_start(b2_d, b2s[:]).then_inc(d_b2, 16)
            sp.wait_ge(d_b2, 16)
            sp.wait_ge(d_pad, 32)

            def P(s, p):
                k = p // CH + XSLOTS
                if p % CH == CH - 1 and (k < CHUNKS or steps_left[0]):
                    sp.wait_ge(s_pooled, s * PARTS + PARTS + p + 1)
                    load_chunk(s + 1 + k // CHUNKS, k % CHUNKS)

            def load_rows(j, buf, listed):
                wait_first(sp, s_pick, j + 1)
                e = sp.value_load(seli[0:1, buf, 0:1], min_val=0, max_val=NE - 1)
                row = sp.value_load(seli[0:1, buf, 1:2], min_val=0, max_val=IDLE)
                sp.wait_ge(s_free, j + 1)
                sp.wait_ge(s_listed, listed)
                w = d_rows[buf]
                sp.dma_start(xr[:, buf], rows_d[bass.ds(row, T)]
                             .rearrange("(p n) c -> p n c", n=TP)).then_inc(w, 16)
                sp.dma_start(b1s[:, buf], b1[bass.ds(e, 1)]
                             .rearrange("b p m -> p (b m)")).then_inc(w, 16)
                sp.dma_start(b2t[:, buf], b2_d[bass.ds(e, 1)]
                             .rearrange("b k c -> k (b c)")).then_inc(w, 16)

            def load_w1(j, buf, first=False):
                e = sp.value_load(seli[0:1, buf, 0:1], min_val=0, max_val=NE - 1)
                if not first:
                    sp.wait_ge(s_w1l, 2 * j)
                for dst, src in ((w1r[:, 0], w1[bass.ds(e, 1), 0:128]), (w1r[0:KB1, 1], w1[bass.ds(e, 1), 128:E]),
                                 (w1r[KB1:128, 1], w1[bass.ds(e, 1), 128:E])):
                    sp.dma_start(dst, src.rearrange("b p f -> p (b f)")).then_inc(d_w1, 16)

            def load_w2(j, buf, first=False):
                e = sp.value_load(seli[0:1, buf, 0:1], min_val=0, max_val=NE - 1)
                if not first:
                    sp.wait_ge(s_w2l, 2 * j)
                sp.dma_start(w2r[:], w2[bass.ds(e, 1)].rearrange("b (m p) f -> p (b m) f", p=128)).then_inc(d_w2, 16)

            listed = [None]
            steps_left = [True]

            def L(j, b):
                load_rows(j + 2, (b + 2) % 3, listed[0])

            def J(j, b):
                load_w1(j + 2, (b + 2) % 3)

            def K(j, b):
                load_w2(j + 1, (b + 1) % 3)

            def S10(s):
                sp.wait_ge(s_h1, s * IPS + IPS)
                for hf in range(2):
                    sp.dma_start(outv[bass.ds(s * IPS, IPS), :, hf].rearrange("b p e -> p b e"),
                                 h1s[:, hf * IPS:(hf + 1) * IPS, 0:E]).then_inc(d_h1, 16)

            handlers = {"P": P, "L": L, "J": J, "K": K, "S10": S10}
            with sp.Fori(0, PRO) as s:
                tiles_do(sp, handlers, s=s, with_tiles=False)
            load_rows(0, 0, PRO + 1)
            load_w1(0, 0, first=True)
            load_w2(0, 0, first=True)
            load_rows(1, 1, PRO + 1)
            load_w1(1, 1)
            with sp.Fori(PRO, STEPS - 2) as s:
                listed[0] = s + 1
                tiles_do(sp, handlers, s=s, j=(s - PRO) * TILES_PER_STEP)
            steps_left[0] = False
            for s in (STEPS - 2, STEPS - 1):
                listed[0] = s + 1
                tiles_do(sp, handlers, s=s, j=(s - PRO) * TILES_PER_STEP, pooling=s < STEPS - 1)
            sp.wait_ge(s_ends, 1)
            for e in range(NE):
                end = sp.value_load(endi[0:1, e:e + 1], min_val=e * CAP,
                                    max_val=e * CAP + TOKENS)
                sp.dma_start(rows_d[bass.ds(end, T)].rearrange("(p n) c -> p n c", n=TP), pad[:]).then_inc(d_pad, 16)
            sp.wait_ge(d_pad, 32 + 16 * NE)
            listed[0] = STEPS + 1
            with sp.Fori(0, TAIL) as i:
                tiles_do(sp, handlers, j=i * TILES_PER_STEP + (STEPS - PRO) * TILES_PER_STEP, with_step=False)
            sp.wait_ge(s_free, 3 + TILES)
            sp.wait_ge(d_w2, 16 * (TILES + 1))
            sp.wait_ge(d_w1, 48 * (TILES + 2))
            for buf in range(3):
                sp.wait_ge(d_rows[buf], 48 * ((TILES + 4 - buf) // 3))

        @block.gpsimd
        def _(pool):
            pool.sem_inc(s_stored, 1)
            pool.sem_inc(s_listed, 1)
            pool.sem_inc(s_free, 2)
            given("pool", "zeros", nc.gpsimd.memset(pad[:], 0.0))
            nc.gpsimd.memset(phi[:, :, 0:1], 1.0)
            nc.gpsimd.memset(att[:, :, ATT - 1:ATT], 1.0)
            nc.gpsimd.memset(mask[:], 0.0)
            nc.gpsimd.memset(ones[:], 1.0)
            nc.gpsimd.memset(cwT[:, :, 0:1], 0.0)
            given("pool", "fills", nc.gpsimd.memset(rstd1[:], 1.0))
            pool.wait_ge(d_w, 16 * 9)
            set_wait(pool, "pool", "zeros")
            given("pool", "pad", nc.gpsimd.tensor_copy(pad[:, :, ROW - 1:ROW].bitcast(I32), padi[:].unsqueeze(2)))

            def Q(s, q):
                if q == 0:
                    wait_first(pool, s_norm, s * 4 + 4)
                    wait_first(pool, s_slots, s + 1)
                for t in (2 * q, 2 * q + 1):
                    for k in range(2):
                        pool.indirect_dma_start(
                            rows_d, bass.IndirectOffsetOnAxis(ap=sloti[:, k * NT + t:k * NT + t + 1], axis=0),
                            rows[:, t, :], None).then_inc(d_scat, 16)
                if q == 3:
                    pool.wait_ge(d_scat, s * (32 * NT) + 32 * NT)
                    pool.wait_ge(d_h1, s * 32 + 32)
                    pool.sem_inc(s_stored, 1)
                    pool.sem_inc(s_listed, 1)

            def A(j, b):
                wait_first(pool, s_ys, j * TP + 2 * TP)
                for n in range(TP):
                    pool.indirect_dma_start(
                        out, bass.IndirectOffsetOnAxis(ap=xr[:, b, n, ROW - 1:ROW].bitcast(I32), axis=0),
                        ys[:, b, n, :], None, compute_op=ALU.add).then_inc(d_add, 16)

            def F(j, b):
                pool.wait_ge(d_add, j * (16 * TP) + 2 * 16 * TP)
                pool.sem_inc(s_free, 1)

            def W(j, b, q):
                cols = slice(q * FF // 2, (q + 1) * FF // 2)
                pool.wait_ge(s_w1h, j * 2 + 3 + q)
                nc.gpsimd.tensor_tensor(w1l[:, :, cols], w1r[:, :, cols], w1h[:, :, cols].bitcast(F32),
                                        ALU.subtract).then_inc(s_w1l, 1)

            def Z(j, b, q):
                pool.wait_ge(s_w2h, j * 2 + (3, 2)[q])
                nc.gpsimd.tensor_tensor(w2l[:, 3 * q:3 * q + 3], w2r[:, 3 * q:3 * q + 3], w2h[:, 3 * q:3 * q + 3].bitcast(F32),
                                ALU.subtract).then_inc(s_w2l, 1)

            def prime():
                wait_first(pool, d_pad, 32)
                for n in range(TP):
                    pool.indirect_dma_start(
                        out, bass.IndirectOffsetOnAxis(ap=padi[:, n:n + 1], axis=0),
                        pad[:, n, 0:E], None, compute_op=ALU.add).then_inc(d_add, 16)
                W(-1, -1, 0)
                W(-1, -1, 1)
                Z(-1, -1, 0)

            schedule(pool, {"Q": Q, "A": A, "F": F, "W": W, "Z": Z}, prime=prime)
            F(TILES - 1, TILES - 1)

        @block.scalar
        def _(act):
            copy = nc.scalar.copy
            act.sem_inc(s_ys, TP)
            act.sem_inc(s_hT, 1)
            set_wait(act, "pe", "turned")
            turned = ps[0:KH, 1, 0:4 * KA].rearrange("p (a k) -> p a k", a=4)
            copy(resT[:, 0:2, :], turned[:, 0:2, :])
            given("act", "resT", copy(resT[:, 2:4, 0:KB], turned[:, 2:4, 0:KB]))
            set_wait(act, "pe", "logits")
            copy(resA[:, E:RES], ps[0:KA, 3, 0:NE])
            given("act", "logits", copy(resB[:, E:RES], ps[0:KB, 3, NE:2 * NE]))
            set_wait(act, "pe", "values")
            given("act", "values", copy(wv3[:, :, 0:HD], ps[0:U, 4, 0:E].rearrange("p (h d) -> p h d", h=HEADS)))
            set_wait(act, "pe", "qk")
            given("act", "qk", copy(qk[:].rearrange("p a h u -> p (a h u)"), ps[0:HD, 5, 0:2 * HEADS * U]))
            set_wait(act, "pe", "bmat")
            given("act", "bmat", copy(bmat.rearrange("p (a b) f -> p a (b f)", b=2), ps[0:U, 0:6, 0:4 * NF]))
            for h in range(HEADS):
                set_wait(act, "pe", f"factors{h}")
                if h >= 2:
                    set_wait(act, "dve", f"score{h - 2}")
                given("act", f"factors{h}", copy(afac[:, h % 2], factors(h)[:, 1]))

            def S1(s):
                act.wait_ge(s_psum1, s + 1)
                copy(pT[:].rearrange("p i j -> p j i"),
                     ps[0:IPS * C, 0, 0:NTOK].rearrange("p (j i) -> p j i", j=G)).then_inc(s_pT, 1)

            def S3(s):
                act.wait_ge(s_g, s + 1)
                copy(gts[:].rearrange("p i f -> p (i f)"), ps[0:U, 0, 0:IPS * NF]).then_inc(s_gts, 1)
                act.wait_ge(s_phT, s + 1)
                copy(phiT[:].rearrange("p (a b) -> p a b", a=2), ps[0:NF, 1:3, 0:IPS * TOK]).then_inc(s_phTs, 1)

            def S4(s):
                act.wait_ge(s_gw, s + 1)
                copy(gws[:].rearrange("p (a b) v -> p a (b v)", a=2), ps[0:NF, 0:2, 0:2 * NV]).then_inc(s_gws, 1)

            def S5(s):
                act.wait_ge(s_u, s + 1)
                hh = HEADS // 2
                w = hh * IPS * HV
                copy(us[:, 0:hh].rearrange("p h i v -> p (h i v)"), ps[0:NF, 2, 0:w])
                copy(us[:, hh:HEADS].rearrange("p h i v -> p (h i v)"), ps[0:NF, 0, 0:w]).then_inc(s_us, 1)

            def S7(s, g):
                act.wait_ge(s_turn, s * 4 + 2 * g + 1)
                copy(attA[:, g * IPS * TOK:(g + 1) * IPS * TOK],
                     ps[0:KA, TURN[2 * g], 0:IPS * TOK]).then_inc(s_tA, 1)

            def S8(s, q):
                if q == 0:
                    act.wait_ge(s_stored, s + 1)
                act.wait_ge(s_res, s * 4 + q + 1)
                copy(h1s[:, 2 * q:2 * q + 2, :],
                     ps[0:TOK, RESB[q], 0:2 * RES].rearrange("p (a r) -> p a r", a=2)).then_inc(s_h1, 1)

            def V(s, q):
                if q == 0:
                    act.wait_ge(s_gap, s + 1)
                    nc.scalar.activation(th[:], gap[:], ACT.Tanh, scale=0.5).then_inc(s_th, 1)
                    act.wait_ge(s_listed, s + 1)
                for t in (2 * q, 2 * q + 1):
                    last = nc.scalar.activation(rows[:, t, 0:E], h1s[:, t, 0:E], ACT.Identity,
                                                bias=shift2[:, t:t + 1], scale=rstd2[:, t:t + 1])
                last.then_inc(s_norm, 1)

            def M(j, b, m):
                act.wait_ge(s_h, j * MC + m + 1)
                act.wait_ge(s_hl, j * MC + m + 1)
                act.wait_ge(s_n, j * MC + m + 1)
                for dst in (hh[:, m % 3, :], hf[:, m % 2, :]):
                    last = nc.scalar.activation(dst, ps[:, HB[m], :], ACT.Gelu, bias=b1s[:, b, m:m + 1])
                last.then_inc(s_hT, 1)

            def W(j, b, q, first=False):
                cols = slice(q * FF // 2, (q + 1) * FF // 2)
                if not first:
                    act.wait_ge(s_h, j * MC + 3 * q + 3)
                if q == 0:
                    act.wait_ge(d_w1, j * 48 + 96)
                copy(w1h[:, :, cols], w1r[:, :, cols]).then_inc(s_w1h, 1)

            def Z(j, b, q, first=False):
                nj = j + 1 - q
                if q == 0:
                    act.wait_ge(d_w2, nj * 16 + 16)
                if not first:
                    act.wait_ge(s_n, nj * MC + 3 * q)
                copy(w2h[:, 3 * q:3 * q + 3], w2r[:, 3 * q:3 * q + 3]).then_inc(s_w2h, 1)

            def X(j, b, q):
                nb = (b + 1) % 3
                act.wait_ge(s_xt, j * 2 + q + 3)
                if q == 0:
                    copy(xh[:, nb], ps[:, XB[0], :]).then_inc(s_xa, 1)
                else:
                    copy(xb[KB1:128, nb], ps[KB1:128, XB[1], :]).then_inc(s_xa, 1)

            def Y(j, b):
                act.wait_ge(s_gate, j + 1)
                for i in range(TP):
                    if i == 0:
                        act.wait_ge(s_y, j + 1)
                    elif i == 2:
                        act.wait_ge(s_n, j * MC + MC + 3)
                    nc.scalar.activation(ys[:, b, i, :], yout(i), ACT.Copy,
                                         scale=gate[:, b, i:i + 1]).then_inc(s_ys, 1)

            def prime():
                W(-1, -1, 0, first=True)
                W(-1, -1, 1, first=True)
                X(-1, -1, 0)
                X(-1, -1, 1)
                Z(-1, -1, 0, first=True)

            schedule(act, {"S1": S1, "S3": S3, "S4": S4, "S5": S5, "S7": S7, "S8": S8, "V": V, "M": M, "W": W, "Z": Z,
                           "X": X, "Y": Y}, prime=prime)

        @block.tensor
        def _(pe):
            mm = nc.tensor.matmul
            ident = const("ident")
            pe.sem_inc(s_n, 3)

            def turn(dst, src):
                n = src.shape[0]
                return nc.tensor.transpose(dst, src, ident[0:n, 0:n])

            set_wait(pe, "dve", "router")
            for hf in range(2):
                cols = slice(hf * KH, (hf + 1) * KH)
                turn(ps[0:KH, 0, hf * C:(hf + 1) * C], cwc[:, cols])
                turn(ps[0:KH, 0, 64 + hf * NE:64 + (hf + 1) * NE], rts[:, cols])
                turn(ps[0:KH, 1, hf * KA:hf * KA + KA], resA[:, cols])
                last = turn(ps[0:KH, 1, (2 + hf) * KA:(2 + hf) * KA + KB], resB[:, cols])
            given("pe", "turned", last)
            set_wait(pe, "pool", "fills")
            set_wait(pe, "dve", "cwT")
            for hf in range(2):
                last = mm(ps[0:C, 2, 0:C], cwT[:, hf, 1:U], cwT[:, hf, 1:U], start=hf == 0, stop=hf == 1)
            given("pe", "gram", last)
            set_wait(pe, "dve", "gram")
            given("pe", "wide", mm(ps[0:C, 2, 64:64 + IPS * C], gram[:, 0:C], const("spread", C),
                                   start=True, stop=True))
            set_wait(pe, "dve", "wide")
            given("pe", "blocks", mm(ps[0:IPS * C, 2, 128:128 + IPS * C], const("spread", C), gram[:, C:C + IPS * C],
                                     start=True, stop=True))
            set_wait(pe, "dve", "rtT")
            set_wait(pe, "act", "resT")
            for r, k in ((0, KA), (1, KB)):
                for hf in range(2):
                    last = mm(ps[0:k, 3, r * NE:(r + 1) * NE], resT[:, 2 * r + hf, 0:k], rtT[:, hf, :],
                              start=hf == 0, stop=hf == 1)
            given("pe", "logits", last)
            for hf in range(2):
                last = mm(ps[0:U, 4, 0:E], cwT[:, hf, :], wqkv[:, hf, 2 * E:3 * E], start=hf == 0, stop=hf == 1)
            given("pe", "values", last)
            for a in range(2):
                for h in range(HEADS):
                    o = (a * HEADS + h) * U
                    for hf in range(2):
                        last = mm(ps[0:HD, 5, o:o + U], wqkv[:, hf, a * E + h * HD:a * E + (h + 1) * HD],
                                  cwT[:, hf, :], start=hf == 0, stop=hf == 1)
            given("pe", "qk", last)
            set_wait(pe, "act", "qk")
            for h in range(HEADS):
                last = mm(ps[0:U, 6, h * U:(h + 1) * U], qk[:, 0, h, :], qk[:, 1, h, :], start=True, stop=True)
            given("pe", "amat", last)
            set_wait(pe, "dve", "amat")
            for h in range(HEADS):
                last = mm(ps[0:U, h // 2, (h % 2) * 2 * NF:(h % 2 + 1) * 2 * NF], amat[:, h, :],
                          const("self", U), start=True, stop=True)
            given("pe", "bmat", last)
            set_wait(pe, "act", "bmat")
            selg = const("selg", U)
            for h in range(HEADS):
                if h >= 6:
                    set_wait(pe, "dve", f"score{h - 6}")
                for k in range(4):
                    last = mm(ps[0:NF, h % 6, k * NF:(k + 1) * NF], selg[:, k * NF:(k + 1) * NF],
                              bmat[:, h, (k % 2) * NF:(k % 2 + 1) * NF], start=True, stop=True)
                given("pe", f"factors{h}", last)
            set_wait(pe, "dve", "b2")

            def S1(s):
                pe.wait_ge(s_pooled, s * PARTS + PARTS)
                lhs = red[:].rearrange("p i c j -> p (i c) j")
                for jj in range(G):
                    last = mm(ps[0:IPS * C, 0, jj * G:(jj + 1) * G], lhs[:, :, jj], const("rowsel", ROWP),
                              start=True, stop=True)
                last.then_inc(s_psum1, 1)

            def S2(s):
                pe.wait_ge(s_pT, s + 1)
                for hf in range(2):
                    last = mm(ps[0:TOK, 1, hf * 96:(hf + 1) * 96],
                              pT[:, hf * G // 2:(hf + 1) * G // 2, :].rearrange("p i j -> p (i j)"), mix,
                              start=True, stop=True)
                last.then_inc(s_mix, 1)

            def S3(s):
                pe.wait_ge(s_phi, s + 1)
                for i in range(IPS):
                    for hf in range(2):
                        t = hf * IPS + i
                        last = mm(ps[0:U, 0, i * NF:(i + 1) * NF], phi[:, t, 0:U], phi[:, t, :],
                                  start=hf == 0, stop=hf == 1)
                last.then_inc(s_g, 1)
                for t in range(NT):
                    last = turn(ps[0:NF, 1 + t // IPS, (t % IPS) * TOK:(t % IPS + 1) * TOK], phi[:, t, :])
                last.then_inc(s_phT, 1)

            def S4(s):
                pe.wait_ge(s_gts, s + 1)
                pe.wait_ge(s_phTs, s + 1)
                for i in range(IPS):
                    last = mm(ps[0:NF, i // 2, (i % 2) * NV:(i % 2 + 1) * NV], gts[:, i, :],
                              const("wvinit", U), start=True, stop=True)
                last.then_inc(s_gw, 1)

            def S5(s):
                pe.wait_ge(s_gws, s + 1)
                for h in range(HEADS):
                    w = IPS * HV
                    bank, o = (2, h) if h < HEADS // 2 else (0, h - HEADS // 2)
                    last = mm(ps[0:NF, bank, o * w:(o + 1) * w].rearrange("p (i v) -> p i v", i=IPS),
                              score[:, h, :], gws[:, :, h * HV:(h + 1) * HV], start=True, stop=True)
                last.then_inc(s_u, 1)

            def S6(s, q):
                if q == 0:
                    pe.wait_ge(s_us, s + 1)
                elif q == 3:
                    pe.wait_ge(s_att, s * 4 + 1)
                for t in (2 * q, 2 * q + 1):
                    last = mm(ps[0:TOK, NUMB[q], (t % 2) * NV:(t % 2 + 1) * NV],
                              phiT[:, t * TOK:(t + 1) * TOK], us[:, :, t % IPS, :], start=True, stop=True)
                    if t % 2:
                        last.then_inc(s_num, 1)

            def S7(s, g):
                for c in range(2):
                    k, w, o = 2 * g + c, (KA, KB)[c], (0, KA)[c]
                    pe.wait_ge(s_att, s * 4 + (2, 3, 4, 4)[k])
                    if k == 3:
                        pe.wait_ge(s_tA, s * 2 + 1)
                    for i in range(IPS):
                        last = turn(ps[0:w, TURN[k], i * TOK:(i + 1) * TOK], att[:, g * IPS + i, o:o + w])
                    last.then_inc(s_turn, 1)

            def S8(s, q):
                pe.wait_ge(s_tA, s * 2 + (1, 2, 2, 2)[q])
                pe.wait_ge(s_tB, s * 2 + (1, 1, 2, 2)[q])
                if q == 3:
                    pe.wait_ge(s_h1, s * 4 + 1)
                for t in (2 * q, 2 * q + 1):
                    o = ps[0:TOK, RESB[q], (t % 2) * RES:(t % 2 + 1) * RES]
                    mm(o, attA[:, t * TOK:(t + 1) * TOK], resA[:], start=True, stop=False)
                    last = mm(o, attB[:, t * TOK:(t + 1) * TOK], resB[:], start=False, stop=True)
                last.then_inc(s_res, 1)

            def S9(s):
                pe.wait_ge(s_mask, s + 1)
                w = (NT + 1) * NE
                mm(ps[:, 2, 0:w], tri[:], mask[:], start=True, stop=False)
                for k in range(1, NT + 1):
                    last = mm(ps[:, 2, k * NE:w], ones[:], mask[:, 0:w - k * NE], start=False, stop=k == NT)
                last.then_inc(s_rank, 1)

            def M(j, b, m):
                if m % 3 == 0:
                    pe.wait_ge(s_w1l, j * 2 + 1 + m // 3)
                if m == 0:
                    pe.wait_ge(s_xd, j * 2 + 2)
                elif m == 5:
                    pe.wait_ge(s_xd, j * 2 + 3)
                elif m == 1:
                    pe.wait_ge(s_hT, j * MC + 1)
                elif m >= 3:
                    pe.wait_ge(s_hT, j * MC + (2, 4)[m - 3])
                cols = slice(m * 128, (m + 1) * 128)
                parts = [(w1h[:, 0, cols], xh[:, b]), (w1h[:, 0, cols], xl[:, b]), (w1l[:, 0, cols], xh[:, b]),
                         (w1h[:, 1, cols], xb[:, b]), (w1l[KB1:128, 1, cols], xb[KB1:128, b])]
                for i, (w, r) in enumerate(parts):
                    last = mm(ps[:, HB[m], :], w, r, start=i == 0, stop=i == len(parts) - 1)
                last.then_inc(s_h, 1)

            def X(j, b, q, first=False):
                nb = (b + 1) % 3
                if q == 0:
                    pe.wait_ge(d_rows[nb], tile_landed(j + 1, nb))
                if not first:
                    pe.wait_ge(s_hT, j * MC + (3, 5)[q])
                for n in range(TP):
                    last = turn(ps[:, XB[q], n * 128:(n + 1) * 128], xr[:, nb, n, q * KB1:q * KB1 + 128])
                last.then_inc(s_xt, 1)

            def N(j, b, m):
                if m % 3 == 0:
                    pe.wait_ge(s_w2l, j * 2 + 1 + m // 3)
                for n in range(TP):
                    cols = slice(n * 128, (n + 1) * 128)
                    if m == 0 and n % 2 == 0:
                        pe.wait_ge(s_ys, j * TP + n + 2)
                        mm(ps[:, 6 + n // 2, 0:2 * E].rearrange("p (a e) -> p a e", a=2), ones[0:3, :],
                           b2t[:, b, :].unsqueeze(1).to_broadcast([3, 2, E]), start=True, stop=False)
                    if n == 0:
                        pe.wait_ge(s_hl, j * MC + m + 3)
                    mm(yout(n), hh[:, m % 3, cols], w2h[:, m, :], start=False, stop=False)
                    mm(yout(n), hh[:, m % 3, cols], w2l[:, m, :], start=False, stop=False)
                    last = mm(yout(n), hl[:, m % 3, cols], w2h[:, m, :], start=False,
                              stop=m == MC - 1 and n % 2 == 1)
                    if m == MC - 1 and n == 1:
                        last.then_inc(s_y, 1)
                last.then_inc(s_n, 1)

            def prime():
                X(-1, -1, 0, first=True)
                X(-1, -1, 1, first=True)

            schedule(pe, {"S1": S1, "S2": S2, "S3": S3, "S4": S4, "S5": S5, "S6": S6, "S7": S7, "S8": S8,
                          "S9": S9, "M": M, "X": X, "N": N}, prime=prime)

        @block.vector
        def _(dve):
            V = nc.vector
            links = {"step": 45, "pick": 9, "gate": 1}
            own_sem = {"step": s_dve, "pick": s_dvp, "gate": s_dvg}
            pos_ = {k: 0 for k in links}

            def mark(ins, kind="step"):
                pos_[kind] += 1
                return ins.then_inc(own_sem[kind], 1)

            def own(i, kind="step", alone=False):
                wait = wait_first if alone else type(dve).wait_ge
                wait(dve, own_sem[kind], i * links[kind] + pos_[kind])

            def bc(ap, n):
                return ap.unsqueeze(len(ap.shape)).to_broadcast(list(ap.shape) + [n])

            def P(s, p, first=False):
                k, c = p // CH, p % CH
                if p == 0 and not first:
                    dve.wait_ge(s_psum1, s + 1)
                if c == 0:
                    dve.wait_ge(d_x[k % XSLOTS], (s + 1) * (16 * CHUNKS // XSLOTS) + 16 * (k // XSLOTS) + 16)
                V.tensor_reduce(red[:, k // 2, CH * (k % 2) + c, :],
                                xbuf[:, k % XSLOTS, c, :].rearrange("p (r j w) -> p j r w", r=2, j=G),
                                AX.XY, ALU.add).then_inc(s_pooled, 1)

            dve.sem_inc(s_hl, 2)
            n_set = [0]

            def link(ins):
                n_set[0] += 1
                ins.then_inc(s_dvs, 1)
                dve.wait_ge(s_dvs, n_set[0])

            dve.wait_ge(d_cst, 16)
            V.tensor_copy(base[:], const("base"))
            V.tensor_copy(cons[:], const("base"))
            V.tensor_copy(ids[:], const("ids", TOK))
            given("dve", "copies", V.tensor_copy(tri[:], const("tri", TOK)))
            dve.wait_ge(d_w, 16 * 9)
            link(V.tensor_reduce(small[:, 0:1], cws[:], AX.X, ALU.add))
            link(V.tensor_scalar(small[:, 1:2], small[:, 0:1], -1.0 / E, None, ALU.mult))
            given("dve", "cwc", V.tensor_scalar(cwc[:], cws[:], small[:, 1:2], None, ALU.add))
            link(V.tensor_reduce(smallr[:, 0:1], rts[:], AX.X, ALU.add))
            link(V.tensor_scalar(smallr[:, 1:2], smallr[:, 0:1], -1.0 / E, None, ALU.mult))
            given("dve", "router", V.tensor_scalar(rts[:], rts[:], smallr[:, 1:2], None, ALU.add))
            set_wait(dve, "pe", "turned")
            given("dve", "cwT", V.tensor_copy(cwT[:, :, 1:U], ps[0:KH, 0, 0:2 * C].rearrange("p (a c) -> p a c", a=2)))
            given("dve", "rtT", V.tensor_copy(rtT[:], ps[0:KH, 0, 64:64 + 2 * NE].rearrange("p (a c) -> p a c", a=2)))
            set_wait(dve, "pe", "gram")
            given("dve", "gram", V.tensor_scalar(gram[:, 0:C], ps[0:C, 2, 0:C], 1.0 / E, None, ALU.mult))
            set_wait(dve, "pe", "wide")
            given("dve", "wide", V.tensor_copy(gram[:, C:C + IPS * C], ps[0:C, 2, 64:64 + IPS * C]))
            set_wait(dve, "pe", "blocks")
            given("dve", "mix", V.tensor_tensor(mix[:, IPS * C:2 * IPS * C], ps[0:IPS * C, 2, 128:128 + IPS * C],
                                                const("block", IPS * C), ALU.mult))
            set_wait(dve, "pe", "amat")
            given("dve", "amat", V.scalar_tensor_tensor(
                out=amat[:], in0=ps[0:U, 6, 0:HEADS * U].rearrange("p (h u) -> p h u", h=HEADS), scalar=HD ** -0.5,
                in1=const("e00", U).unsqueeze(1).to_broadcast([U, HEADS, U]), op0=ALU.mult, op1=ALU.add))
            set_wait(dve, "pool", "fills")
            for h in range(HEADS):
                for p in range(PARTS * h // HEADS, PARTS * (h + 1) // HEADS):
                    P(-1, p, first=True)
                set_wait(dve, "act", f"factors{h}")
                if h:
                    set_wait(dve, "dve", f"score{h - 1}")
                link(V.tensor_tensor(atmp[:], factors(h)[:, 0], afac[:, h % 2], ALU.mult))
                given("dve", f"score{h}", V.tensor_tensor(score[:, h, :], atmp[:, 0], atmp[:, 1], ALU.add))
            set_wait(dve, "dve", f"score{HEADS - 1}")
            given("dve", "score", V.tensor_scalar(score[0:1, :, 0:1], score[0:1, :, 0:1], 0.5, None, ALU.add))
            link(V.tensor_copy(b2s[:, 0], b2f[:, 0]))
            link(V.tensor_tensor(b2f[:, 1], b2f[:, 0], b2s[:, 0], ALU.subtract))
            link(V.tensor_copy(b2s[:, 1], b2f[:, 1]))
            link(V.tensor_tensor(b2f[:, 0], b2f[:, 1], b2s[:, 1], ALU.subtract))
            given("dve", "b2", V.tensor_copy(b2s[:, 2], b2f[:, 0]))

            def inverse_root(s, y, v):
                mark(V.tensor_scalar(y.bitcast(I32), v.bitcast(I32), -0.5, float(0x5f3759df), ALU.mult, ALU.add))
                own(s)
                for _ in range(3):
                    mark(V.tensor_tensor(newton[:, 0], y, y, ALU.mult))
                    own(s)
                    mark(V.scalar_tensor_tensor(out=newton[:, 1], in0=newton[:, 0], scalar=-0.5, in1=v,
                                                op0=ALU.mult, op1=ALU.mult))
                    own(s)
                    mark(V.scalar_tensor_tensor(out=y, in0=newton[:, 1], scalar=1.5, in1=y,
                                                op0=ALU.add, op1=ALU.mult))
                    own(s)

            att_ch = att[:, :, E:E + C]

            def S2(s):
                dve.wait_ge(s_mix, s + 1)
                mixed = ps[0:TOK, 1, 0:192].rearrange("p (a b c) -> p a b c", a=2, b=2 * IPS)
                att4 = att_ch.rearrange("p (a b) c -> p a b c", a=2)
                mark(V.tensor_copy(att4, mixed[:, :, 0:IPS]))
                own(s)
                mark(V.tensor_tensor(prod[:].rearrange("p (a b) c -> p a b c", a=2), att4, mixed[:, :, IPS:2 * IPS],
                                     ALU.mult))
                own(s)
                mark(V.tensor_reduce(var1[:], prod[:], AX.X, ALU.add))
                own(s)
                mark(V.tensor_scalar(var1[:], var1[:], EPS, None, ALU.add))
                own(s)
                inverse_root(s, rstd1[:], var1[:])
                mark(V.tensor_tensor(phi[:, :, 1:U], att_ch, bc(rstd1[:], C), ALU.mult))
                own(s)
                for i in range(1, U):
                    last = V.tensor_tensor(phi[:, :, FOFF[i]:FOFF[i] + U - i], phi[:, :, i:U],
                                           phi[:, :, i:i + 1].to_broadcast([TOK, NT, U - i]), ALU.mult)
                last.then_inc(s_phi, 1)

            def S6(s, q):
                dve.wait_ge(s_num, s * 4 + q + 1)
                num = ps[0:TOK, NUMB[q], 0:2 * NV].rearrange("p (a h v) -> p a h v", a=2, h=HEADS)
                if q:
                    dve.wait_ge(s_att, s * 4 + q)
                mark(V.reciprocal(rden[:].unsqueeze(3), num[:, :, :, HD:HV]))
                own(s)
                V.tensor_tensor(att[:, 2 * q:2 * q + 2, 0:E].rearrange("p a (h d) -> p a h d", h=HEADS),
                                num[:, :, :, 0:HD], bc(rden[:], HD), ALU.mult).then_inc(s_att, 1)

            def S7(s, g):
                dve.wait_ge(s_turn, s * 4 + 2 * g + 2)
                V.tensor_copy(attB[:, g * IPS * TOK:(g + 1) * IPS * TOK],
                              ps[0:KB, TURN[2 * g + 1], 0:IPS * TOK]).then_inc(s_tB, 1)

            def S8(s, q):
                dve.wait_ge(s_h1, s * 4 + q + 1)
                for t in (2 * q, 2 * q + 1):
                    V.bn_stats(stats[:, t, :], h1s[:, t, 0:E])
                    last = V.max(top[:, t, :], h1s[:, t, E:RES])
                mark(last)

            def S10(s):
                own(s, alone=True)
                for t in range(NT):
                    V.bn_aggr(mv[:, t, :], stats[:, t, :])
                    last = V.max_index(topi[:, t, :], top[:, t, :], h1s[:, t, E:RES])
                mark(last)
                own(s, alone=True)
                V.tensor_scalar(var2[:].unsqueeze(2), mv[:, :, 1:2], EPS, None, ALU.add)
                V.tensor_tensor(gap[:].unsqueeze(2), top[:, :, 0:1], top[:, :, 1:2], ALU.subtract)
                mark(V.tensor_copy(idxf[:].rearrange("p k t -> p t k"), topi[:, :, 0:2]))
                own(s)
                mark(V.tensor_tensor(hot[:], bc(idxf[:].rearrange("p k t -> p (k t)"), NE),
                                     const("iota", TOK).unsqueeze(1).to_broadcast([TOK, 2 * NT, NE]), ALU.is_equal))
                own(s)
                V.tensor_tensor(mask[:, 0:NT * NE].rearrange("p (t e) -> p t e", t=NT), hot[:, 0:NT, :],
                                hot[:, NT:2 * NT, :], ALU.add).then_inc(s_mask, 1)

            def R(s):
                inverse_root(s, rstd2[:], var2[:])
                V.scalar_tensor_tensor(out=shift2[:].unsqueeze(2), in0=mv[:, :, 0:1], scalar=-1.0,
                                       in1=rstd2[:].unsqueeze(2), op0=ALU.mult, op1=ALU.mult)
                V.tensor_tensor(gap[:], gap[:], rstd2[:], ALU.mult).then_inc(s_gap, 1)

            def S11(s):
                dve.wait_ge(s_listed, s + 1)
                mark(V.tensor_copy(rows[:, :, ROW - 1:ROW].bitcast(I32), ids[:].unsqueeze(2)))
                own(s)
                mark(V.tensor_scalar(ids[:], ids[:], float(IPS * NTOK), None, ALU.add))
                dve.wait_ge(s_th, s + 1)
                V.tensor_scalar(gk[:, 0], th[:], 0.5, 0.5, ALU.mult, ALU.add)
                mark(V.tensor_scalar(gk[:, 1], th[:], -0.5, 0.5, ALU.mult, ALU.add))
                own(s)
                mark(V.tensor_tensor(hotw[:], hot[:], bc(gk[:].rearrange("p k t -> p (k t)"), NE), ALU.mult))
                own(s)
                mark(V.tensor_tensor(rows[:, :, E:E + NE], hotw[:, 0:NT, :], hotw[:, NT:2 * NT, :], ALU.add))

            def S9(s):
                dve.wait_ge(s_rank, s + 1)
                own(s)
                mark(V.tensor_tensor(pos[:].rearrange("p (t e) -> p t e", t=NT),
                                ps[0:TOK, 2, 0:NT * NE].rearrange("p (t e) -> p t e", t=NT),
                                base[0:TOK].unsqueeze(1).to_broadcast([TOK, NT, NE]), ALU.add))
                own(s)
                mark(V.tensor_tensor(base[:], ps[:, 2, NT * NE:(NT + 1) * NE], base[:], ALU.add))
                own(s)
                mark(V.tensor_tensor(hotw[:].rearrange("p (k t) e -> p k (t e)", k=2),
                                     hot[:].rearrange("p (k t) e -> p k (t e)", k=2),
                                     pos[:].unsqueeze(1).to_broadcast([TOK, 2, NT * NE]), ALU.mult))
                own(s)
                mark(V.tensor_reduce(slotf[:], hotw[:], AX.X, ALU.add))
                own(s)
                V.tensor_copy(sloti[:], slotf[:]).then_inc(s_slots, 1)
                assert pos_["step"] == links["step"], pos_

            def count_rows(n):
                V.tensor_copy(avail[:], base[:]).then_inc(s_avail, 1)
                wait_first(dve, s_avail, n)

            primed = []

            def S1(s):
                pos_["step"] = 0
                if primed:
                    count_rows(s - PRO + 2)

            def L(j, b):
                nb = (b + 2) % 3
                pos_["pick"] = 0

                def then(ins, alone=False):
                    mark(ins, "pick")
                    own(j + 2, "pick", alone)

                then(V.tensor_tensor(pend[:], avail[:], cons[:], ALU.subtract), alone=True)
                then(V.max(pmax[:], pend[:]), alone=True)
                then(V.max_index(pidx[:], pmax[:], pend[:]))
                V.tensor_copy(pick[:, 0:1], pidx[:, 0:1])
                then(V.tensor_scalar(pick[:, 1:2], pmax[:, 0:1], 0.0, None, ALU.is_le))
                then(V.tensor_scalar(hotE[:, nb], const("iota"), pick[:, 0:1], None, ALU.is_equal))
                then(V.tensor_tensor(tmpE[:], hotE[:, nb], cons[:], ALU.mult))
                V.tensor_reduce(pick[:, 2:3], tmpE[:], AX.X, ALU.add)
                then(V.scalar_tensor_tensor(out=cons[:], in0=hotE[:, nb], scalar=float(T), in1=cons[:],
                                            op0=ALU.mult, op1=ALU.add))
                then(V.tensor_scalar(pick[:, 3:4], pick[:, 2:3], -1.0, float(IDLE), ALU.mult, ALU.add))
                then(V.scalar_tensor_tensor(out=pick[:, 4:5], in0=pick[:, 3:4], scalar=pick[:, 1:2],
                                            in1=pick[:, 2:3], op0=ALU.mult, op1=ALU.add))
                V.tensor_copy(seli[0:1, nb, 0:1], pick[0:1, 0:1])
                V.tensor_copy(seli[0:1, nb, 1:2], pick[0:1, 4:5]).then_inc(s_pick, 1)
                assert pos_["pick"] == links["pick"], pos_

            def X(j, b, q, first=False):
                nb = (b + 1) % 3
                if q == 0:
                    dve.wait_ge(s_xa, j * 2 + 3)
                    V.tensor_tensor(xl[:, nb], ps[:, XB[0], :], xh[:, nb].bitcast(F32), ALU.subtract).then_inc(s_xd, 1)
                    dve.wait_ge(d_rows[nb], tile_landed(j + 1, nb))
                    if not first:
                        dve.wait_ge(s_gate, j + 1)
                    mark(V.tensor_tensor(gmul[:], xr[:, nb, :, E:E + NE],
                                         hotE[:, nb].unsqueeze(1).to_broadcast([128, TP, NE]), ALU.mult), "gate")
                    pos_["gate"] = 1
                    own(j + 1, "gate")
                    V.tensor_reduce(gate[:, nb], gmul[:], AX.X, ALU.add).then_inc(s_gate, 1)
                else:
                    dve.wait_ge(s_xa, j * 2 + 4)
                    V.tensor_tensor(xb[0:KB1, nb], ps[KB1:128, XB[1], :], xb[KB1:128, nb].bitcast(F32),
                                    ALU.subtract).then_inc(s_xd, 1)

            def M(j, b, m):
                dve.wait_ge(s_hT, j * MC + m + 2)
                V.tensor_tensor(hl[:, m % 3, :], hf[:, m % 2, :], hh[:, m % 3, :].bitcast(F32),
                                ALU.subtract).then_inc(s_hl, 1)

            def prime():
                primed.append(True)
                count_rows(1)
                L(-2, -2)
                L(-1, -1)
                X(-1, -1, 0, first=True)
                X(-1, -1, 1)

            def list_ends():
                V.tensor_copy(endi[:], base[0:1, :]).then_inc(s_ends, 1)
                count_rows(STEPS - PRO + 2)

            schedule(dve, {"P": P, "S1": S1, "S2": S2, "S6": S6, "S7": S7, "S8": S8, "S10": S10, "R": R,
                           "S11": S11, "S9": S9, "L": L, "M": M, "X": X},
                     prime=prime, before_tail=list_ends)
    return nc


_INS = ["x", "L0_tok_channel_weights", "L0_attn_w_qkv", "L0_attn_w_proj", "L0_attn_b_proj", "L0_ffn_router_w",
        "L0_ffn_w1", "L0_ffn_b1", "L0_ffn_w2", "L0_ffn_b2"]


def kernel(**inputs):
    import concourse.bacc as bacc
    from concourse.bass_utils import run_bass_kernel_spmd as run

    nc = bacc.Bacc("TRN2", target_bir_lowering=False, num_devices=1)
    arrays, args = {}, []

    def give(name, a):
        arrays[name] = np.ascontiguousarray(a)
        args.append(nc.dram_tensor(name, arrays[name].shape, mybir.dt.from_np(arrays[name].dtype),
                                   kind="ExternalInput").ap())

    for name in _INS:
        a = np.asarray(inputs[name])
        if name == "L0_ffn_b1":
            a = a.reshape(NE, MC, 128).transpose(0, 2, 1)
        give(name, a)
    for name, a in zip(("consts", "padids"), constants()):
        give(name, a)
    args.append(nc.dram_tensor("result", (TOKENS + T, E), F32, kind="ExternalOutput").ap())
    vit_layer(nc, *args)
    got = run(nc, [arrays], core_ids=[0]).results[0]["result"]
    return got[:TOKENS].reshape(B, NTOK, E)
```
